# Optimizing a Trainium2 kernel written in Bass

```python
import numpy as np
import jax
import jax.numpy as jnp

def _softmax(x, axis=-1):
    return jax.nn.softmax(x, axis=axis)

def _gelu(x):
    return jax.nn.gelu(x, approximate=True)

def _silu(x):
    return jax.nn.silu(x)

def _sigmoid(x):
    return jax.nn.sigmoid(x)

def _layernorm(x, axis=-1, eps=1e-05):
    m = jnp.mean(x, axis=axis, keepdims=True)
    v = jnp.var(x, axis=axis, keepdims=True)
    return (x - m) / jnp.sqrt(v + eps)

def _scatter_add(tgt, idx, src, axis=0):
    return tgt.at[idx].add(src)

def _segment_sum(src, seg, n):
    return jax.ops.segment_sum(src, seg, n)
kernel_name = 'mk_audio_tower_d1_tok_audfeat256_r4_5d9e00'

def setup_inputs(seed: int=0):
    np.random.seed(seed)
    _w = jnp.asarray

    def _rec_inputs():
        import jax
        import jax.numpy as jnp
        _rk = jax.random.key(seed)
        x = -0.000392918 + 0.999932 * jax.random.normal(jax.random.fold_in(_rk, 1), (8, 750, 128), jnp.float32)
        return x
    x = _rec_inputs()

    def _L0_tok_setup():
        import jax, jax.numpy as jnp
        from jax import lax
        import numpy as np
        BN_EPS = 0.001

        @jax.custom_vjp
        def ste_sign(x):
            return jnp.where(x >= 0, 1.0, -1.0).astype(x.dtype)

        def _ste_fwd(x):
            return (ste_sign(x), x)

        def _ste_bwd(x, g):
            return (g * (jnp.abs(x) <= 1.0).astype(g.dtype),)
        ste_sign.defvjp(_ste_fwd, _ste_bwd)
        key = jax.random.key(seed)
        ks = jax.random.split(key, 6)
        x = jax.random.normal(ks[0], (64, 512, 128), dtype=jnp.float32)
        kernel = jax.random.normal(ks[1], (3, 128, 64), dtype=jnp.float32) * 0.05
        bias = jax.random.normal(ks[2], (64,), dtype=jnp.float32) * 0.01
        beta = jax.random.normal(ks[3], (64,), dtype=jnp.float32) * 0.01
        moving_mean = jax.random.normal(ks[4], (64,), dtype=jnp.float32) * 0.1
        moving_var = jax.random.uniform(ks[5], (64,), dtype=jnp.float32) + 0.5
        return {'x': x, 'kernel': kernel, 'bias': bias, 'beta': beta, 'moving_mean': moving_mean, 'moving_var': moving_var}
    _L0_tok_all = _L0_tok_setup()
    _L0_tok_in = {k: v for k, v in _L0_tok_all.items() if k in ('kernel', 'bias', 'beta', 'moving_mean', 'moving_var')}
    del _L0_tok_all

    def _L0_attn_setup():
        import jax, jax.numpy as jnp
        import numpy as np
        import math
        D_MODEL = 64
        NHEAD = 8
        D_LATTICE = 512
        D_K = D_LATTICE // NHEAD
        PHI = (1.0 + math.sqrt(5.0)) / 2.0
        PHI_INV = 1.0 / PHI
        PHI_INT = 1618.0
        C1 = PHI * math.sqrt(2.0) * 51.85
        C2 = math.pi / PHI

        def qrt_damping(x):
            return jnp.sin(C1 * x) * jnp.exp(-(x * x) / PHI) + jnp.cos(C2 * x)

        def ttt_filter(scores):
            int_scores = (jnp.abs(scores) * PHI_INT).astype(jnp.int32)
            mod9 = int_scores % 9
            chaos = (mod9 == 0) | (mod9 == 3) | (mod9 == 6)
            penalty = jnp.where(chaos, jnp.float32(PHI_INV), jnp.float32(1.0))
            return scores * penalty
        key = jax.random.key(seed)
        ks = jax.random.split(key, 9)
        B, S = (2, 512)
        s_in = 1.0 / math.sqrt(D_MODEL)
        s_lat = 1.0 / math.sqrt(D_LATTICE)
        return {'x': jax.random.normal(ks[0], (B, S, D_MODEL), dtype=jnp.float32), 'Wq': jax.random.normal(ks[1], (D_MODEL, D_LATTICE), dtype=jnp.float32) * s_in, 'bq': jax.random.normal(ks[2], (D_LATTICE,), dtype=jnp.float32) * 0.01, 'Wk': jax.random.normal(ks[3], (D_MODEL, D_LATTICE), dtype=jnp.float32) * s_in, 'bk': jax.random.normal(ks[4], (D_LATTICE,), dtype=jnp.float32) * 0.01, 'Wv': jax.random.normal(ks[5], (D_MODEL, D_LATTICE), dtype=jnp.float32) * s_in, 'bv': jax.random.normal(ks[6], (D_LATTICE,), dtype=jnp.float32) * 0.01, 'Wo': jax.random.normal(ks[7], (D_LATTICE, D_MODEL), dtype=jnp.float32) * s_lat, 'bo': jax.random.normal(ks[8], (D_MODEL,), dtype=jnp.float32) * 0.01}
    _L0_attn_all = _L0_attn_setup()
    _L0_attn_in = {k: v for k, v in _L0_attn_all.items() if k in ('Wq', 'bq', 'Wk', 'bk', 'Wv', 'bv', 'Wo', 'bo')}
    del _L0_attn_all

    def _L0_ffn_setup():
        import jax, jax.numpy as jnp
        import numpy as np
        E = 8
        K = 2
        D = 64
        H = 128
        DOUT = 64
        EPS = 1e-05
        key = jax.random.key(seed)
        ks = jax.random.split(key, 9)
        s = 0.02
        return {'x': jax.random.normal(ks[0], (4, 2048, D), jnp.float32), 'gamma': 1.0 + 0.05 * jax.random.normal(ks[1], (D,), jnp.float32), 'beta': 0.05 * jax.random.normal(ks[2], (D,), jnp.float32), 'Wr': 0.01 * jax.random.normal(ks[3], (D, E), jnp.float32), 'br': jnp.zeros((E,), jnp.float32), 'W1': s * jax.random.normal(ks[4], (E, D, H), jnp.float32), 'b1': s * jax.random.normal(ks[5], (E, H), jnp.float32), 'W2': s * jax.random.normal(ks[6], (E, H, DOUT), jnp.float32), 'b2': s * jax.random.normal(ks[7], (E, DOUT), jnp.float32)}
    _L0_ffn_all = _L0_ffn_setup()
    _L0_ffn_in = {k: v for k, v in _L0_ffn_all.items() if k in ('gamma', 'beta', 'Wr', 'br', 'W1', 'b1', 'W2', 'b2')}
    del _L0_ffn_all
    return {'x': x, 'L0_tok_kernel': _L0_tok_in['kernel'], 'L0_tok_bias': _L0_tok_in['bias'], 'L0_tok_beta': _L0_tok_in['beta'], 'L0_tok_moving_mean': _L0_tok_in['moving_mean'], 'L0_tok_moving_var': _L0_tok_in['moving_var'], 'L0_attn_Wq': _L0_attn_in['Wq'], 'L0_attn_bq': _L0_attn_in['bq'], 'L0_attn_Wk': _L0_attn_in['Wk'], 'L0_attn_bk': _L0_attn_in['bk'], 'L0_attn_Wv': _L0_attn_in['Wv'], 'L0_attn_bv': _L0_attn_in['bv'], 'L0_attn_Wo': _L0_attn_in['Wo'], 'L0_attn_bo': _L0_attn_in['bo'], 'L0_ffn_gamma': _L0_ffn_in['gamma'], 'L0_ffn_beta': _L0_ffn_in['beta'], 'L0_ffn_Wr': _L0_ffn_in['Wr'], 'L0_ffn_br': _L0_ffn_in['br'], 'L0_ffn_W1': _L0_ffn_in['W1'], 'L0_ffn_b1': _L0_ffn_in['b1'], 'L0_ffn_W2': _L0_ffn_in['W2'], 'L0_ffn_b2': _L0_ffn_in['b2']}

def reference(x, L0_tok_kernel, L0_tok_bias, L0_tok_beta, L0_tok_moving_mean, L0_tok_moving_var, L0_attn_Wq, L0_attn_bq, L0_attn_Wk, L0_attn_bk, L0_attn_Wv, L0_attn_bv, L0_attn_Wo, L0_attn_bo, L0_ffn_gamma, L0_ffn_beta, L0_ffn_Wr, L0_ffn_br, L0_ffn_W1, L0_ffn_b1, L0_ffn_W2, L0_ffn_b2):
    import jax
    import jax.numpy as jnp

    def _L0_tok_ref(x, kernel, bias, beta, moving_mean, moving_var):
        import jax, jax.numpy as jnp
        from jax import lax
        import numpy as np
        BN_EPS = 0.001

        @jax.custom_vjp
        def ste_sign(x):
            return jnp.where(x >= 0, 1.0, -1.0).astype(x.dtype)

        def _ste_fwd(x):
            return (ste_sign(x), x)

        def _ste_bwd(x, g):
            return (g * (jnp.abs(x) <= 1.0).astype(g.dtype),)
        ste_sign.defvjp(_ste_fwd, _ste_bwd)
        xq = ste_sign(x)
        kq = ste_sign(kernel)
        y = lax.conv_general_dilated(xq, kq, window_strides=(1,), padding='VALID', dimension_numbers=('NWC', 'WIO', 'NWC'))
        y = y + bias
        inv = lax.rsqrt(moving_var + BN_EPS)
        return (y - moving_mean) * inv + beta

    def _L0_attn_ref(x, Wq, bq, Wk, bk, Wv, bv, Wo, bo):
        import jax, jax.numpy as jnp
        import numpy as np
        import math
        D_MODEL = 64
        NHEAD = 8
        D_LATTICE = 512
        D_K = D_LATTICE // NHEAD
        PHI = (1.0 + math.sqrt(5.0)) / 2.0
        PHI_INV = 1.0 / PHI
        PHI_INT = 1618.0
        C1 = PHI * math.sqrt(2.0) * 51.85
        C2 = math.pi / PHI

        def qrt_damping(x):
            return jnp.sin(C1 * x) * jnp.exp(-(x * x) / PHI) + jnp.cos(C2 * x)

        def ttt_filter(scores):
            int_scores = (jnp.abs(scores) * PHI_INT).astype(jnp.int32)
            mod9 = int_scores % 9
            chaos = (mod9 == 0) | (mod9 == 3) | (mod9 == 6)
            penalty = jnp.where(chaos, jnp.float32(PHI_INV), jnp.float32(1.0))
            return scores * penalty
        B, S, _ = x.shape

        def split_heads(t):
            return t.reshape(B, S, NHEAD, D_K).transpose(0, 2, 1, 3)
        q = split_heads(x @ Wq + bq)
        k = split_heads(x @ Wk + bk)
        v = split_heads(x @ Wv + bv)
        scores = jnp.einsum('bhqd,bhkd->bhqk', q, k) / jnp.float32(math.sqrt(D_K))
        scores = ttt_filter(scores)
        attn = jax.nn.softmax(scores, axis=-1)
        attn = attn * qrt_damping(attn)
        ctx = jnp.einsum('bhqk,bhkd->bhqd', attn, v)
        ctx = ctx.transpose(0, 2, 1, 3).reshape(B, S, D_LATTICE)
        return ctx @ Wo + bo

    def _L0_ffn_ref(x, gamma, beta, Wr, br, W1, b1, W2, b2):
        import jax, jax.numpy as jnp
        import numpy as np
        E = 8
        K = 2
        D = 64
        H = 128
        DOUT = 64
        EPS = 1e-05
        mu = jnp.mean(x, axis=-1, keepdims=True)
        var = jnp.mean(jnp.square(x - mu), axis=-1, keepdims=True)
        xn = (x - mu) * jax.lax.rsqrt(var + EPS) * gamma + beta
        logits = jnp.einsum('bsd,de->bse', xn, Wr) + br
        top_vals, top_idx = jax.lax.top_k(logits, K)
        w = jax.nn.softmax(top_vals, axis=-1)
        w_full = jnp.einsum('bsk,bske->bse', w, jax.nn.one_hot(top_idx, E, dtype=w.dtype))
        y = jnp.zeros(x.shape[:-1] + (DOUT,), x.dtype)
        for e in range(E):
            h = jax.nn.gelu(jnp.einsum('bsd,dh->bsh', xn, W1[e]) + b1[e], approximate=False)
            y_e = jnp.einsum('bsh,hd->bsd', h, W2[e]) + b2[e]
            y = y + y_e * w_full[..., e, None]
        return y
    h = _L0_tok_ref(x, L0_tok_kernel, L0_tok_bias, L0_tok_beta, L0_tok_moving_mean, L0_tok_moving_var)
    h = h + _L0_attn_ref(_layernorm(h, axis=-1), L0_attn_Wq, L0_attn_bq, L0_attn_Wk, L0_attn_bk, L0_attn_Wv, L0_attn_bv, L0_attn_Wo, L0_attn_bo)
    h = h + _L0_ffn_ref(_layernorm(h, axis=-1), L0_ffn_gamma, L0_ffn_beta, L0_ffn_Wr, L0_ffn_br, L0_ffn_W1, L0_ffn_b1, L0_ffn_W2, L0_ffn_b2)
    return h

_drawn_inputs = setup_inputs


def setup_inputs(seed=0):
    import zlib

    import numpy as np

    out = dict(_drawn_inputs(seed))
    spreads = {'L0_ffn_br': (0.0, 0.8)}
    factors = {'L0_tok_bias': 8.0,
     'L0_tok_beta': 8.0,
     'L0_tok_moving_mean': 8.0,
     'L0_attn_Wq': 5.522,
     'L0_attn_bq': 8.0,
     'L0_attn_Wk': 5.595,
     'L0_attn_bk': 8.0,
     'L0_attn_Wv': 5.457,
     'L0_attn_bv': 32.074,
     'L0_attn_Wo': 5.411,
     'L0_attn_bo': 64.0,
     'L0_ffn_gamma': 8.0,
     'L0_ffn_beta': 8.0,
     'L0_ffn_Wr': 8.0,
     'L0_ffn_W1': 8.0,
     'L0_ffn_b1': 64.0,
     'L0_ffn_W2': 8.0,
     'L0_ffn_b2': 64.0}
    for name, (base, spread) in spreads.items():
        noise = np.random.default_rng([zlib.crc32(name.encode()), seed]).standard_normal(out[name].shape)
        drawn = base * np.exp(spread * noise) if base else spread * noise
        out[name] = jnp.asarray(drawn.astype(out[name].dtype))
    for name, factor in factors.items():
        out[name] = (out[name] * factor).astype(out[name].dtype)
    return out
```

```python
import math
from contextlib import ExitStack

import numpy as np

import concourse.bass as bass
from concourse import mybir

F32 = mybir.dt.float32
BF16 = mybir.dt.bfloat16
I32 = mybir.dt.int32
U32 = mybir.dt.uint32
ALU = mybir.AluOpType
ACT = mybir.ActivationFunctionType
AX = mybir.AxisListType

B = 8
S_IN = 750
TAPS = 3
S = S_IN - TAPS + 1
C_IN = 128
D = 64
HEADS = 8
DK = 64
LAT = HEADS * DK
P = 128
TILES = -(-S // P)
STRIDE = (S - P) // (TILES - 1)
assert STRIDE * (TILES - 1) + P == S
TAIL = P - STRIDE
EXPERTS = 8
HID = 128
CAND = 8
HIGH_BITS = ~0xFFF
M_PROJ = 1.5 * 2.0 ** 8
M_SCORE = 1.5 * 2.0 ** 11
BN_EPS = 1e-3
LN_EPS = 1e-5


def wait_alone(engine, semaphore, value, passed):
    engine.wait_ge(semaphore, value)
    engine.sem_inc(passed, 1)


def tokens_and_projections(nc, a, s):
    with ExitStack() as ctx:
        def sb(name, shape, dt=F32):
            return ctx.enter_context(nc.sbuf_tensor("a_" + name, shape, dt))

        def sem(name):
            return ctx.enter_context(nc.semaphore("a_" + name))

        x_t = sb("x_t", [C_IN, 2, P + TAPS - 1])
        x_sign = sb("x_sign", [C_IN, P + TAPS - 1], BF16)
        k_raw = sb("k_raw", [C_IN, TAPS, D])
        k_sign = sb("k_sign", [C_IN, TAPS, D], BF16)
        w_qk = sb("w_qk", [P, 2 * LAT])
        w_a = sb("w_a", [P, 2 * LAT])
        w_b = sb("w_b", [P, 2 * LAT])
        w_v = sb("w_v", [P, LAT])
        b_qk = sb("b_qk", [P, 2 * LAT])
        b_v = sb("b_v", [P, LAT])
        vec = sb("vec", [P, 3, D])
        ident = sb("ident", [P, P])
        row_mask = sb("row_mask", [P, D + 2])
        m_col = sb("m_col", [P, 1])
        ones = sb("ones", [P, P])
        var_col = sb("var_col", [D, 12])
        inv = sb("inv", [P, D])
        inv_diag = sb("inv_diag", [D, D])
        h = sb("h", [P, D])
        red = sb("red", [P, 64])
        col = sb("col", [P, 16])
        dev = sb("dev", [P, D])
        sq = sb("sq", [P, D])
        q0 = sb("q0", [P, D])
        q_hi = sb("q_hi", [P, D])
        q_lo = sb("q_lo", [P, D])
        z_cat = sb("z_cat", [P, 2, D])
        z_t = sb("z_t", [P, P])
        z_row = sb("z_row", [P, 2, P])
        grid_a = sb("grid_a", [P, 2, 2 * LAT])
        grid_acc = sb("grid_acc", [P, 2 * LAT])
        low_a = sb("low_a", [P, 2 * LAT])
        low_acc = sb("low_acc", [P, 2 * LAT])
        high = sb("high", [P, 2 * LAT])
        acc = sb("acc", [P, 2 * LAT])
        qk = sb("qk", [P, 2 * LAT])
        v = sb("v", [P, LAT])
        ps = ctx.enter_context(nc.psum_tensor("a_ps", [P, 8, 512], F32))
        ps_conv = ps[:, 0, 0:D]
        ps_zt = ps[:, 1, 0:P]
        ps_v = ps[:, 2, :]
        ps_inv = ps[:, 3, 0:D]

        def prod_a(slot):
            return ps[:, 4 * slot:4 * slot + 2, :]

        def prod_b(slot):
            return ps[:, 4 * slot + 2:4 * slot + 4, :]

        def banked(t):
            return t.rearrange("p (a n) -> p a n", a=2)

        consts_in = sem("consts_in")
        x_in = [sem(f"x_in{j}") for j in range(2)]
        ident_ready = sem("ident_ready")
        w_split = sem("w_split")
        rs_dve = sem("rs_dve")
        rs_act = sem("rs_act")
        diag_ready = sem("diag_ready")
        inv_ready = sem("inv_ready")
        sign_ready = sem("sign_ready")
        conv_ready = sem("conv_ready")
        var_ready = sem("var_ready")
        root_ready = sem("root_ready")
        z_ready = sem("z_ready")
        zt_psum = sem("zt_psum")
        zt_ready = sem("zt_ready")
        v_psum = sem("v_psum")
        v_ready = sem("v_ready")
        row_ready = sem("row_ready")
        prod_ready = sem("prod_ready")
        prod_free = sem("prod_free")
        ga_ready = sem("ga_ready")
        gacc_ready = sem("gacc_ready")
        acc_ready = sem("acc_ready")
        qk_ready = sem("qk_ready")
        stored = sem("stored")
        passed = sem("passed")
        STORES = 4 * 16
        STORES_B = STORES * (TILES + 1)

        block = ctx.enter_context(nc.Block())

        @block.sync
        def _(sp):
            for dst, src in ((k_raw[:, :, :], a["kernel"].rearrange("w c d -> c w d")),
                             (w_qk[0:D, 0:LAT], a["Wq"]), (w_qk[D:P, 0:LAT], a["Wq"]),
                             (w_qk[0:D, LAT:], a["Wk"]), (w_qk[D:P, LAT:], a["Wk"]),
                             (w_v[0:D, :], a["Wv"]), (w_v[D:P, :], a["Wv"]),
                             (b_qk[:, 0:LAT], a["bq"].partition_broadcast(P)),
                             (b_qk[:, LAT:], a["bk"].partition_broadcast(P)),
                             (b_v[:, :], a["bv"].partition_broadcast(P)),
                             (vec[:, 0, :], a["bias"].partition_broadcast(P)),
                             (vec[:, 1, :], a["moving_mean"].partition_broadcast(P)),
                             (vec[:, 2, :], a["beta"].partition_broadcast(P)),
                             (var_col[:, 0:1], a["moving_var"].rearrange("(d o) -> d o", o=1))):
                sp.dma_start(dst, src).then_inc(consts_in, 16)
            with sp.Fori(0, B) as b:
                with sp.Fori(0, TILES // 2) as tt:
                    for j in range(2):
                        n = b * TILES + tt * 2 + j
                        t = tt * 2 + j
                        row = t * STRIDE
                        sp.wait_ge(qk_ready, n + 1)
                        sp.wait_ge(v_ready, n + 1)
                        sp.dma_start(s["h"][b, bass.ds(row, STRIDE), :], h[0:STRIDE, :]).then_inc(stored, 16)
                        sp.dma_start(s["q"][b, :, bass.ds(row, STRIDE), :].rearrange("h r d -> r h d"),
                                     qk[0:STRIDE, 0:LAT].rearrange("r (h d) -> r h d", h=HEADS)).then_inc(stored, 16)
                        sp.dma_start(s["kv"][b, :, bass.ds(row, STRIDE), 0:DK].rearrange("h r d -> r h d"),
                                     qk[0:STRIDE, LAT:].rearrange("r (h d) -> r h d", h=HEADS)).then_inc(stored, 16)
                        sp.dma_start(s["kv"][b, :, bass.ds(row, STRIDE), DK:].rearrange("h r d -> r h d"),
                                     v[0:STRIDE, :].rearrange("r (h d) -> r h d", h=HEADS)).then_inc(stored, 16)
                sp.dma_start(s["h"][b, S - TAIL:S, :], h[STRIDE:P, :]).then_inc(stored, 16)
                sp.dma_start(s["q"][b, :, S - TAIL:S, :].rearrange("h r d -> r h d"),
                             qk[STRIDE:P, 0:LAT].rearrange("r (h d) -> r h d", h=HEADS)).then_inc(stored, 16)
                sp.dma_start(s["kv"][b, :, S - TAIL:S, 0:DK].rearrange("h r d -> r h d"),
                             qk[STRIDE:P, LAT:].rearrange("r (h d) -> r h d", h=HEADS)).then_inc(stored, 16)
                sp.dma_start(s["kv"][b, :, S - TAIL:S, DK:].rearrange("h r d -> r h d"),
                             v[STRIDE:P, :].rearrange("r (h d) -> r h d", h=HEADS)).then_inc(stored, 16)
            sp.wait_ge(stored, B * STORES_B)

        @block.gpsimd
        def _(gp):
            gp.memset(ident[:, :], 0.0)
            gp.memset(row_mask[:, :], 0.0)
            gp.memset(ones[:, :], 1.0)
            gp.memset(m_col[:, :], M_PROJ).then_inc(ident_ready, 1)
            gp.drain()
            gp.wait_ge(ident_ready, 1)
            gp.affine_select(out=ident[:, :], in_=ident[:, :], compare_op=ALU.not_equal, fill=1.0,
                             base=0, pattern=[[-1, P]], channel_multiplier=1)
            gp.affine_select(out=row_mask[:, :], in_=row_mask[:, :], compare_op=ALU.not_equal, fill=1.0,
                             base=0, pattern=[[-1, D + 2]], channel_multiplier=1).then_inc(ident_ready, 1)
            gp.wait_ge(ident_ready, 2)
            gp.affine_select(out=row_mask[:, :], in_=row_mask[:, :], compare_op=ALU.not_equal, fill=1.0,
                             base=-D, pattern=[[-1, D + 2]], channel_multiplier=1).then_inc(ident_ready, 1)
            for j in range(2):
                gp.dma_start(x_t[:, j, :], a["x_tiles"][j, :, :]).then_inc(x_in[j], 16)
            with gp.Fori(0, B * TILES // 2 - 1) as pair:
                for j in range(2):
                    gp.wait_ge(sign_ready, pair * 2 + j + 1)
                    gp.dma_start(x_t[:, j, :], a["x_tiles"][bass.ds(pair * 2 + j + 2, 1), :, :]
                                 .rearrange("o c r -> (o c) r")).then_inc(x_in[j], 16)

        def tile_prologue(dve, b, tt, j, n):
            def c(i):
                return col[:, i:i + 1]

            def split(hi, lo, x):
                dve.tensor_scalar(hi.bitcast(I32), x.bitcast(I32), HIGH_BITS, None, ALU.bitwise_and)
                dve.drain()
                dve.tensor_tensor(lo, x, hi, ALU.subtract)
                dve.drain()

            dve.wait_ge(x_in[j], (b * (TILES // 2) + tt) * 16 + 16)
            dve.tensor_scalar(x_sign[:, :], x_t[:, j, :], 0.0, 0.5, ALU.is_ge, ALU.subtract).then_inc(sign_ready, 1)
            dve.wait_ge(stored, b * STORES_B + (tt * 2 + j) * STORES)
            dve.wait_ge(conv_ready, n + 1)
            dve.scalar_tensor_tensor(h[:, :], ps_conv, 4.0, vec[:, 0, :], ALU.mult, ALU.add)
            dve.drain()
            dve.tensor_tensor(h[:, :], h[:, :], vec[:, 1, :], ALU.subtract)
            dve.drain()
            dve.tensor_tensor(h[:, :], h[:, :], inv[:, :], ALU.mult)
            dve.drain()
            dve.tensor_tensor(h[:, :], h[:, :], vec[:, 2, :], ALU.add)
            dve.drain()
            dve.tensor_tensor(red[:, 0:16], h[:, 0:16], h[:, 16:32], ALU.add)
            dve.drain()
            dve.tensor_tensor(red[:, 0:16], red[:, 0:16], h[:, 32:48], ALU.add)
            dve.drain()
            dve.tensor_tensor(red[:, 0:16], red[:, 0:16], h[:, 48:64], ALU.add)
            dve.drain()
            lanes = red[:, 0:16].rearrange("p (a b c) -> p a b c", a=2, b=2)
            dve.tensor_tensor(red[:, 16:24].rearrange("p (a c) -> p a c", a=2), lanes[:, :, 0, :],
                              lanes[:, :, 1, :], ALU.add)
            dve.drain()
            dve.tensor_tensor(red[:, 24:28], red[:, 16:20], red[:, 20:24], ALU.add)
            dve.drain()
            dve.tensor_tensor(red[:, 28:30], red[:, 24:28:2], red[:, 25:28:2], ALU.add)
            dve.drain()
            dve.tensor_tensor(c(0), red[:, 28:29], red[:, 29:30], ALU.add)
            dve.drain()
            dve.tensor_scalar(c(0), c(0), 1.0 / D, None, ALU.mult)
            dve.drain()
            dve.tensor_scalar(dev[:, :], h[:, :], c(0), None, ALU.subtract)
            dve.drain()
            dve.tensor_tensor(sq[:, :], dev[:, :], dev[:, :], ALU.mult)
            dve.drain()
            dve.tensor_reduce(red[:, 32:34], sq[:, :].rearrange("p (a n) -> p a n", a=2), AX.X, ALU.add)
            dve.drain()
            dve.tensor_tensor(c(1), red[:, 32:33], red[:, 33:34], ALU.add)
            dve.drain()
            dve.tensor_scalar(c(1), c(1), 1.0 / D, LN_EPS, ALU.mult, ALU.add).then_inc(var_ready, 1)
            dve.wait_ge(root_ready, n + 1)
            dve.reciprocal(c(3), c(2))
            split(c(4), c(5), c(2))
            dve.tensor_tensor(c(6), c(4), c(4), ALU.mult)
            dve.drain()
            dve.tensor_tensor(c(6), c(1), c(6), ALU.subtract)
            dve.tensor_tensor(c(7), c(4), c(5), ALU.mult)
            dve.drain()
            dve.scalar_tensor_tensor(c(6), c(7), -2.0, c(6), ALU.mult, ALU.add)
            dve.drain()
            dve.tensor_tensor(c(7), c(5), c(5), ALU.mult)
            dve.drain()
            dve.tensor_tensor(c(6), c(6), c(7), ALU.subtract)
            dve.drain()
            dve.scalar_tensor_tensor(c(6), c(6), 0.5, c(3), ALU.mult, ALU.mult)
            dve.drain()
            dve.tensor_tensor(c(2), c(2), c(6), ALU.add)
            dve.drain()
            dve.reciprocal(c(3), c(2))
            split(c(4), c(5), c(2))
            dve.tensor_scalar(q0[:, :], dev[:, :], c(3), None, ALU.mult)
            dve.drain()
            split(q_hi[:, :], q_lo[:, :], q0[:, :])
            dve.tensor_scalar(c(6), c(4), -1.0, None, ALU.mult)
            dve.tensor_scalar(c(7), c(5), -1.0, None, ALU.mult)
            dve.drain()
            for part, scal in ((q_hi, c(6)), (q_hi, c(7)), (q_lo, c(6)), (q_lo, c(7))):
                dve.scalar_tensor_tensor(dev[:, :], part[:, :], scal, dev[:, :], ALU.mult, ALU.add)
                dve.drain()
            dve.scalar_tensor_tensor(q0[:, :], dev[:, :], c(3), q0[:, :], ALU.mult, ALU.add)
            dve.drain()
            dve.tensor_scalar(z_cat[:, 0, :].bitcast(I32), q0[:, :].bitcast(I32), HIGH_BITS, None, ALU.bitwise_and)
            dve.drain()
            dve.tensor_tensor(z_cat[:, 1, :], q0[:, :], z_cat[:, 0, :], ALU.subtract).then_inc(z_ready, 1)
            dve.memset(acc[:, :], 0.0).then_inc(acc_ready, 1)
            dve.wait_ge(v_psum, n + 1)
            dve.tensor_tensor(v[:, :], ps_v, b_v[:, :], ALU.add).then_inc(v_ready, 1)

        @block.vector
        def _(dve):
            def split(hi, lo, x):
                dve.tensor_scalar(hi.bitcast(I32), x.bitcast(I32), HIGH_BITS, None, ALU.bitwise_and)
                dve.drain()
                dve.tensor_tensor(lo, x, hi, ALU.subtract)
                dve.drain()

            dve.wait_ge(consts_in, 14 * 16)
            dve.tensor_scalar(k_sign[:, :, :], k_raw[:, :, :], 0.0, 0.5, ALU.is_ge, ALU.subtract)
            dve.memset(w_a[D:P, :], 0.0)
            dve.tensor_copy(w_b[D:P, :], w_qk[D:P, :])
            split(w_a[0:D, :], w_b[0:D, :], w_qk[0:D, :])

            def c(n):
                return var_col[:, n:n + 1]
            dve.tensor_scalar(c(1), c(0), BN_EPS, None, ALU.add)
            dve.drain()
            dve.tensor_scalar(c(2).bitcast(I32), c(1).bitcast(I32), ~0x1FFF, 0x1000, ALU.bitwise_and,
                              ALU.bitwise_or).then_inc(rs_dve, 1)
            dve.wait_ge(rs_act, 1)
            dve.reciprocal(c(4), c(3))
            dve.drain()
            for _ in range(2):
                dve.tensor_tensor(c(5), c(4), c(4), ALU.mult)
                dve.drain()
                dve.tensor_tensor(c(5), c(5), c(2), ALU.mult)
                dve.drain()
                dve.tensor_scalar(c(5), c(5), -0.5, 1.5, ALU.mult, ALU.add)
                dve.drain()
                dve.tensor_tensor(c(4), c(4), c(5), ALU.mult)
                dve.drain()
            dve.tensor_scalar(c(5), c(4), 2.0 ** 11 + 1, None, ALU.mult)
            dve.drain()
            dve.tensor_tensor(c(6), c(5), c(4), ALU.subtract)
            dve.drain()
            dve.tensor_tensor(c(6), c(5), c(6), ALU.subtract)
            dve.drain()
            for i in range(2):
                dve.tensor_tensor(c(7), c(1), c(6), ALU.mult)
                dve.tensor_scalar(c(8), c(6), -0.5, None, ALU.mult).then_inc(rs_dve, 1)
                dve.wait_ge(rs_act, 2 + i)
                dve.tensor_copy(c(6), c(10))
                dve.drain()
            dve.wait_ge(ident_ready, 3)
            dve.tensor_scalar(inv_diag[:, :], ident[0:D, 0:D], c(6), None, ALU.mult).then_inc(diag_ready, 1)
            dve.wait_ge(inv_ready, 1)
            dve.tensor_copy(inv[:, :], ps_inv).then_inc(w_split, 1)

            dve.sem_inc(prod_free, 2)
            with dve.Fori(0, B) as b:
                with dve.Fori(0, TILES // 2) as tt:
                    for j in range(2):
                        n = b * TILES + tt * 2 + j
                        tile_prologue(dve, b, tt, j, n)
                        with dve.Fori(0, D // 2) as kk:
                            for slot in range(2):
                                g = n * D + kk * 2 + slot
                                ga = grid_a[:, slot, :]
                                dve.wait_ge(ga_ready, g + 1)
                                dve.scalar_tensor_tensor(banked(low_a[:, :]), banked(ga), M_PROJ, prod_a(slot),
                                                         ALU.subtract, ALU.subtract, reverse1=True)
                                dve.drain()
                                dve.tensor_tensor(banked(low_a[:, :]), banked(low_a[:, :]), prod_b(slot),
                                                  ALU.add).then_inc(prod_free, 1)
                                dve.wait_ge(gacc_ready, g + 1)
                                dve.scalar_tensor_tensor(low_acc[:, :], grid_acc[:, :], M_PROJ, acc[:, :],
                                                         ALU.subtract, ALU.subtract, reverse1=True)
                                dve.scalar_tensor_tensor(high[:, :], ga, M_PROJ, grid_acc[:, :],
                                                         ALU.subtract, ALU.add)
                                dve.drain()
                                dve.tensor_tensor(low_acc[:, :], low_acc[:, :], low_a[:, :], ALU.add)
                                dve.drain()
                                dve.scalar_tensor_tensor(acc[:, :], high[:, :], M_PROJ, low_acc[:, :],
                                                         ALU.subtract, ALU.add).then_inc(acc_ready, 1)
                                dve.drain()
                        dve.tensor_tensor(qk[:, :], acc[:, :], b_qk[:, :], ALU.add).then_inc(qk_ready, 1)

        @block.scalar
        def _(act):
            def c(n):
                return var_col[:, n:n + 1]
            act.wait_ge(rs_dve, 1)
            act.activation(c(3), c(2), ACT.Sqrt).then_inc(rs_act, 1)
            act.wait_ge(ident_ready, 3)
            act.mul(c(11), ones[0:D, 0:1], -1.0)
            act.drain()
            for i in range(2):
                act.wait_ge(rs_dve, 2 + i)
                act.activation(c(9), c(7), ACT.Identity, bias=c(11), scale=c(6))
                act.drain()
                act.activation(c(10), c(9), ACT.Identity, bias=c(6), scale=c(8)).then_inc(rs_act, 1)
            with act.Fori(0, B) as b:
                with act.Fori(0, TILES) as t:
                    n = b * TILES + t
                    act.wait_ge(var_ready, n + 1)
                    act.activation(col[:, 2:3], col[:, 1:2], ACT.Sqrt).then_inc(root_ready, 1)
                    act.wait_ge(zt_psum, n + 1)
                    act.activation(z_t[:, :], ps_zt, ACT.Copy).then_inc(zt_ready, 1)
                    act.drain()
                    for slot in range(2):
                        act.activation(z_row[:, slot, :], z_t[:, :], ACT.Copy,
                                       scale=row_mask[:, slot:slot + 1]).then_inc(row_ready, 1)
                    with act.Fori(0, D // 2) as kk:
                        for slot in range(2):
                            g = n * D + kk * 2 + slot
                            act.wait_ge(prod_ready, g + 1)
                            act.activation(banked(grid_a[:, slot, :]), prod_a(slot), ACT.Identity,
                                           bias=m_col[:, :]).then_inc(ga_ready, 1)
                            act.activation(z_row[:, slot, :], z_t[:, :], ACT.Copy,
                                           scale=row_mask[:, bass.ds(kk * 2 + slot + 2, 1)]).then_inc(row_ready, 1)
                            act.wait_ge(acc_ready, n * (D + 1) + kk * 2 + slot + 1)
                            act.activation(grid_acc[:, :], acc[:, :], ACT.Identity,
                                           bias=m_col[:, :]).then_inc(gacc_ready, 1)

        @block.tensor
        def _(pe):
            pe.wait_ge(diag_ready, 1)
            pe.matmul(ps_inv, ones[0:D, :], inv_diag[:, :], start=True, stop=True).then_inc(inv_ready, 1)
            pe.wait_ge(w_split, 1)
            with pe.Fori(0, B) as b:
                with pe.Fori(0, TILES) as t:
                    n = b * TILES + t
                    pe.wait_ge(sign_ready, n + 1)
                    pe.wait_ge(prod_free, n * D + 2)
                    for w in range(TAPS):
                        mm = pe.matmul(ps_conv, x_sign[:, w:w + P], k_sign[:, w, :],
                                       start=(w == 0), stop=(w == TAPS - 1))
                    mm.then_inc(conv_ready, 1)
                    wait_alone(pe, z_ready, n + 1, passed)
                    pe.transpose(ps_zt, z_cat[:, :, :].rearrange("p a d -> p (a d)"), ident[:, :]).then_inc(zt_psum, 1)
                    pe.wait_ge(zt_ready, n + 1)
                    pe.matmul(ps_v, z_t[:, :], w_v[:, :], start=True, stop=True).then_inc(v_psum, 1)
                    wait_alone(pe, v_ready, n + 1, passed)
                    with pe.Fori(0, D // 2) as kk:
                        for slot in range(2):
                            k = kk * 2 + slot
                            pe.wait_ge(row_ready, n * (D + 2) + k + 1)
                            pe.wait_ge(prod_free, n * D + k + 1)
                            for half in range(2):
                                pe.matmul(prod_a(slot)[:, half, :], z_row[:, slot, :],
                                          w_a[:, 512 * half:512 * half + 512], start=True, stop=True)
                            for half in range(2):
                                mm = pe.matmul(prod_b(slot)[:, half, :], z_row[:, slot, :],
                                               w_b[:, 512 * half:512 * half + 512], start=True, stop=True)
                            mm.then_inc(prod_ready, 1)


def attention(nc, s):
    PHI = (1.0 + math.sqrt(5.0)) / 2.0
    PHI_INV = float(np.float32(1.0 / PHI))
    TURNS = PHI * math.sqrt(2.0) * 51.85 / (2.0 * math.pi)
    COS = math.pi / PHI
    TWO_PI = float(np.nextafter(np.float32(2.0 * math.pi), np.float32(0)))
    W = S + CAND
    HALF = S // 2
    NEG = -1e9
    with ExitStack() as ctx:
        def sb(name, shape, dt=F32):
            return ctx.enter_context(nc.sbuf_tensor("b_" + name, shape, dt))

        def sem(name):
            return ctx.enter_context(nc.semaphore("b_" + name))

        ident = sb("ident", [P, P])
        q = sb("q", [P, TILES, DK])
        q_hi = sb("q_hi", [P, TILES, DK])
        q_lo = sb("q_lo", [P, TILES, DK])
        kv = sb("kv", [P, TILES, 2 * DK])
        q_t = sb("q_t", [DK, TILES, P])
        k_t = sb("k_t", [DK, S])
        sc = sb("sc", [P, TILES, W])
        top = sb("top", [P, TILES, CAND])
        idx = sb("idx", [P, TILES, CAND], U32)
        row_of = sb("row_of", [P, TILES * CAND], U32)
        base = sb("base", [P, 1])
        kv_c = sb("kv_c", [P, TILES * CAND, 2 * DK])
        k_hi = sb("k_hi", [P, TILES * CAND, DK])
        k_lo = sb("k_lo", [P, TILES * CAND, DK])
        pa = sb("pa", [P, TILES * CAND, DK])
        pb_ = sb("pb", [P, TILES * CAND, DK])
        lanes = sb("lanes", [P, 4, TILES * CAND, 4])
        pair = sb("pair", [P, TILES * CAND, 2])
        w1 = sb("w1", [P, TILES, W])
        w2 = sb("w2", [P, TILES, W])
        wi = sb("wi", [P, TILES, W], I32)
        biases = sb("biases", [P, 3])
        stats = sb("stats", [P, 4, TILES])
        a_t = sb("a_t", [P, 2, 3, P])
        out_c = sb("out_c", [P, TILES, DK])
        out = sb("out", [P, TILES, DK])
        ps = ctx.enter_context(nc.psum_tensor("b_ps", [P, 8, 512], F32))

        ident_ready = sem("ident_ready")
        loaded = sem("loaded")
        tr_psum = sem("tr_psum")
        tr_copied = sem("tr_copied")
        score_psum = sem("score_psum")
        score_copied = sem("score_copied")
        rows_ready = sem("rows_ready")
        gathered = sem("gathered")
        exact_ready = sem("exact_ready")
        trunc_ready = sem("trunc_ready")
        rest_ready = sem("rest_ready")
        dist_ready = sem("dist_ready")
        max_ready = sem("max_ready")
        exp_ready = sem("exp_ready")
        prob_ready = sem("prob_ready")
        turn_ready = sem("turn_ready")
        frac_ready = sem("frac_ready")
        wave_ready = sem("wave_ready")
        weights_ready = sem("weights_ready")
        pv_ready = sem("pv_ready")
        out_ready = sem("out_ready")
        stored = sem("stored")
        passed = sem("passed")
        HEAD_TR = 4 + 2 * TILES

        def block_rows(t):
            return P if t == TILES - 1 else STRIDE

        block = ctx.enter_context(nc.Block())

        @block.sync
        def _(sp):
            with sp.Fori(0, B) as b:
                with sp.Fori(0, HEADS) as hd:
                    n = b * HEADS + hd
                    sp.wait_ge(out_ready, n)
                    for t in range(TILES):
                        sp.dma_start(q[:, t, :], s["q"][b, bass.ds(hd, 1), STRIDE * t:STRIDE * t + P, :]
                                     .rearrange("o r d -> (o r) d")).then_inc(loaded, 16)
                        sp.dma_start(kv[:, t, :], s["kv"][b, bass.ds(hd, 1), STRIDE * t:STRIDE * t + P, :]
                                     .rearrange("o r d -> (o r) d")).then_inc(loaded, 16)
                    sp.wait_ge(out_ready, n + 1)
                    sp.dma_start(s["ctx"][b, 0:STRIDE * TILES, bass.ds(hd * DK, DK)]
                                 .rearrange("(t r) d -> r t d", t=TILES), out[0:STRIDE, :, :]).then_inc(stored, 16)
                    sp.dma_start(s["ctx"][b, S - TAIL:S, bass.ds(hd * DK, DK)],
                                 out[STRIDE:P, TILES - 1, :]).then_inc(stored, 16)
            sp.wait_ge(stored, B * HEADS * 32)

        @block.gpsimd
        def _(gp):
            gp.memset(ident[:, :], 0.0)
            gp.memset(biases[:, 0:1], -1.0 / 3.0)
            gp.memset(biases[:, 1:2], math.pi / 2.0)
            gp.memset(biases[:, 2:3], -(0.5 - 2.0 ** -25))
            gp.memset(base[:, :], 0.0).then_inc(ident_ready, 1)
            gp.wait_ge(ident_ready, 1)
            gp.affine_select(out=ident[:, :], in_=ident[:, :], compare_op=ALU.not_equal, fill=1.0,
                             base=0, pattern=[[-1, P]], channel_multiplier=1).then_inc(ident_ready, 1)
            with gp.Fori(0, B * HEADS) as n:
                wait_alone(gp, rows_ready, n + 1, passed)
                for i in range(TILES * CAND):
                    gp.indirect_dma_start(kv_c[:, i, :], None, s["kv"].rearrange("b h r d -> (b h r) d"),
                                          bass.IndirectOffsetOnAxis(row_of[:, i:i + 1], 0)).then_inc(gathered, 16)

        @block.tensor
        def _(pe):
            pe.wait_ge(ident_ready, 2)
            with pe.Fori(0, B * HEADS) as n:
                pe.wait_ge(loaded, n * (2 * TILES * 16) + 2 * TILES * 16)
                for g in range(4):
                    wait_alone(pe, tr_copied, n * HEAD_TR + max(0, g - 2), passed)
                    for i in range(3):
                        t = 3 * (g % 2) + i
                        src = kv[:, t, 0:DK] if g < 2 else q[:, t, :]
                        mm = pe.transpose(ps[0:DK, 4 + g % 3, P * i:P * i + P], src, ident[:, :])
                    mm.then_inc(tr_psum, 1)
                pe.wait_ge(tr_copied, n * HEAD_TR + 4)
                for t in range(TILES):
                    pe.wait_ge(score_copied, n * TILES + max(0, t - 1))
                    for half in range(2):
                        mm = pe.matmul(ps[:, 2 * (t % 2) + half, 0:HALF], q_t[:, t, :],
                                       k_t[:, HALF * half:HALF * half + HALF], start=True, stop=True)
                    mm.then_inc(score_psum, 1)
                pe.wait_ge(weights_ready, n + 1)

                def turn(g):
                    t, part = g // 2, g % 2
                    pe.wait_ge(tr_copied, n * HEAD_TR + 4 + max(0, g - 2))
                    for i in range(3):
                        k = 3 * part + i
                        mm = pe.transpose(ps[0:block_rows(k), 4 + (g + 4) % 3, P * i:P * i + P],
                                          w1[:, t, STRIDE * k:STRIDE * k + block_rows(k)], ident[:, :])
                    mm.then_inc(tr_psum, 1)

                def weigh(g):
                    t, part = g // 2, g % 2
                    pe.wait_ge(tr_copied, n * HEAD_TR + 4 + g + 1)
                    for i in range(3):
                        k = 3 * part + i
                        mm = pe.matmul(ps[:, 7, DK * t:DK * t + DK], a_t[0:block_rows(k), g % 2, i, :],
                                       kv[0:block_rows(k), k, DK:], start=(k == 0), stop=(k == TILES - 1))
                    if part:
                        mm.then_inc(pv_ready, 1)

                turn(0)
                for g in range(1, 2 * TILES):
                    turn(g)
                    weigh(g - 1)
                weigh(2 * TILES - 1)

        @block.scalar
        def _(act):
            act.wait_ge(ident_ready, 2)
            with act.Fori(0, B * HEADS) as n:
                for g in range(4):
                    act.wait_ge(tr_psum, n * HEAD_TR + g + 1)
                    for i in range(3):
                        t = 3 * (g % 2) + i
                        src = ps[0:DK, 4 + g % 3, P * i:P * i + block_rows(t)]
                        if g < 2:
                            last = act.activation(k_t[:, STRIDE * t:STRIDE * t + block_rows(t)], src, ACT.Copy,
                                                  scale=DK ** -0.5)
                        else:
                            src = ps[0:DK, 4 + g % 3, P * i:P * i + P]
                            last = act.activation(q_t[:, t, :], src, ACT.Copy)
                    last.then_inc(tr_copied, 1)
                for t in range(TILES):
                    act.wait_ge(score_psum, n * TILES + t + 1)
                    act.activation(sc[:, t, 0:S].rearrange("p (a n) -> p a n", a=2),
                                   ps[:, 2 * (t % 2):2 * (t % 2) + 2, 0:HALF], ACT.Copy).then_inc(score_copied, 1)
                act.wait_ge(exact_ready, n + 1)
                act.activation(w1[:, :, :], sc[:, :, :], ACT.Abs, scale=1618.0)
                act.drain()
                act.activation(wi[:, :, :], w1[:, :, :], ACT.Identity, scale=1.0 / 3.0,
                               bias=biases[:, 0:1]).then_inc(trunc_ready, 1)
                act.wait_ge(rest_ready, n + 1)
                act.activation(w1[:, :, :], w1[:, :, :], ACT.Abs, bias=biases[:, 2:3]).then_inc(dist_ready, 1)
                act.wait_ge(max_ready, n + 1)
                for t in range(TILES):
                    last = act.activation(w2[:, t, :], w2[:, t, :], ACT.Exp, bias=stats[:, 1, t:t + 1],
                                          accum_out=stats[:, 2, t:t + 1])
                last.then_inc(exp_ready, 1)
                act.wait_ge(prob_ready, n + 1)
                act.activation(wi[:, :, :], w2[:, :, :], ACT.Copy, scale=TURNS).then_inc(turn_ready, 1)
                act.activation(sc[:, :, :], w2[:, :, :], ACT.Square)
                act.drain()
                act.activation(sc[:, :, :], sc[:, :, :], ACT.Exp, scale=-1.0 / PHI)
                act.wait_ge(frac_ready, n + 1)
                act.activation(w1[:, :, :], w1[:, :, :], ACT.Sin, scale=TWO_PI)
                act.activation(wi[:, :, :].bitcast(F32), w2[:, :, :], ACT.Sin, scale=-COS,
                               bias=biases[:, 1:2]).then_inc(wave_ready, 1)
                for g in range(2 * TILES):
                    t, part = g // 2, g % 2
                    act.wait_ge(tr_psum, n * HEAD_TR + 4 + g + 1)
                    if g >= 4:
                        act.wait_ge(pv_ready, n * TILES + g // 2 - 1)
                    if part == 0:
                        last = act.activation(a_t[0:STRIDE, g % 2, :, :], ps[0:STRIDE, 4 + (g + 4) % 3, 0:3 * P]
                                              .rearrange("p (i n) -> p i n", i=3), ACT.Copy)
                    else:
                        act.activation(a_t[0:STRIDE, g % 2, 0:2, :], ps[0:STRIDE, 4 + (g + 4) % 3, 0:2 * P]
                                       .rearrange("p (i n) -> p i n", i=2), ACT.Copy)
                        last = act.activation(a_t[:, g % 2, 2, :], ps[:, 4 + (g + 4) % 3, 2 * P:3 * P], ACT.Copy)
                    last.then_inc(tr_copied, 1)

        @block.vector
        def _(dve):
            dve.wait_ge(ident_ready, 2)

            def rounded_steps():
                dve.tensor_scalar(q_hi[:, :, :].bitcast(I32), q[:, :, :].bitcast(I32), HIGH_BITS, None,
                                  ALU.bitwise_and)
                dve.tensor_scalar(k_hi[:, :, :].bitcast(I32), kv_c[:, :, 0:DK].bitcast(I32), HIGH_BITS, None,
                                  ALU.bitwise_and)
                dve.drain()
                dve.tensor_tensor(q_lo[:, :, :], q[:, :, :], q_hi[:, :, :], ALU.subtract)
                dve.tensor_tensor(k_lo[:, :, :], kv_c[:, :, 0:DK], k_hi[:, :, :], ALU.subtract)

                def by_row(x):
                    return x.rearrange("p (t c) d -> p t c d", c=CAND)

                def spread(x):
                    return x.unsqueeze(2).broadcast_to([P, TILES, CAND, DK])
                dve.tensor_tensor(by_row(pa[:, :, :]), by_row(k_hi[:, :, :]), spread(q_hi[:, :, :]), ALU.mult)
                dve.drain()
                dve.tensor_tensor(by_row(pb_[:, :, :]), by_row(k_lo[:, :, :]), spread(q_hi[:, :, :]), ALU.mult)
                dve.drain()
                dve.tensor_tensor(by_row(k_lo[:, :, :]), by_row(kv_c[:, :, 0:DK]), spread(q_lo[:, :, :]), ALU.mult)
                dve.tensor_scalar(k_hi[:, :, :], pa[:, :, :], M_SCORE, M_SCORE, ALU.add, ALU.subtract)
                dve.drain()
                dve.tensor_tensor(pb_[:, :, :], pb_[:, :, :], k_lo[:, :, :], ALU.add)
                dve.tensor_tensor(pa[:, :, :], pa[:, :, :], k_hi[:, :, :], ALU.subtract)
                dve.drain()
                dve.tensor_tensor(pa[:, :, :], pa[:, :, :], pb_[:, :, :], ALU.add)
                dve.drain()
                acc, grid, low, high = (lanes[:, i, :, :] for i in range(4))
                dve.tensor_tensor(acc, k_hi[:, :, 0:4], pa[:, :, 0:4], ALU.add)
                dve.drain()
                for j in range(4, DK, 4):
                    dve.tensor_scalar(grid, acc, M_SCORE, M_SCORE, ALU.add, ALU.subtract)
                    dve.drain()
                    dve.tensor_tensor(low, acc, grid, ALU.subtract)
                    dve.tensor_tensor(high, grid, k_hi[:, :, j:j + 4], ALU.add)
                    dve.drain()
                    dve.tensor_tensor(low, low, pa[:, :, j:j + 4], ALU.add)
                    dve.drain()
                    dve.tensor_tensor(acc, high, low, ALU.add)
                    dve.drain()
                dve.tensor_tensor(pair[:, :, :], lanes[:, 0, :, 0:4:2], lanes[:, 0, :, 1:4:2], ALU.add)
                dve.drain()
                dve.tensor_tensor(pair[:, :, 0], pair[:, :, 0], pair[:, :, 1], ALU.add)
                dve.drain()
                dve.tensor_scalar(sc[:, :, S:W], pair[:, :, 0].rearrange("p (t c) -> p t c", c=CAND),
                                  DK ** -0.5, None, ALU.mult).then_inc(exact_ready, 1)

            with dve.Fori(0, B * HEADS) as n:
                for t in range(TILES):
                    wait_alone(dve, score_copied, n * TILES + t + 1, passed)
                    dve.max(top[:, t, :], sc[:, t, 0:S])
                    dve.drain()
                    dve.max_index(idx[:, t, :], top[:, t, :], sc[:, t, 0:S])
                    dve.drain()
                    dve.match_replace(sc[:, t, 0:S], top[:, t, :], sc[:, t, 0:S], NEG)
                dve.drain()
                dve.tensor_scalar(row_of[:, :], idx[:, :, :].rearrange("p t c -> p (t c)"), base[:, :], None,
                                  ALU.add).then_inc(rows_ready, 1)
                dve.drain()
                dve.tensor_scalar(base[:, :], base[:, :], float(S), None, ALU.add)
                dve.wait_ge(gathered, n * (TILES * CAND * 16) + TILES * CAND * 16)
                rounded_steps()
                dve.wait_ge(trunc_ready, n + 1)
                dve.scalar_tensor_tensor(w1[:, :, :], wi[:, :, :], -3.0, w1[:, :, :], ALU.mult,
                                         ALU.add).then_inc(rest_ready, 1)
                dve.wait_ge(dist_ready, n + 1)
                dve.tensor_scalar(w1[:, :, :], w1[:, :, :], 0.5, PHI_INV, ALU.is_ge, ALU.max)
                dve.drain()
                for t in range(TILES):
                    dve.tensor_tensor(w2[:, t, :], w1[:, t, :], sc[:, t, :], ALU.mult)
                dve.drain()
                dve.tensor_reduce(stats[:, 0, :], w2[:, :, :], AX.X, ALU.max)
                dve.drain()
                dve.tensor_scalar(stats[:, 1, :], stats[:, 0, :], -1.0, None, ALU.mult).then_inc(max_ready, 1)
                dve.wait_ge(exp_ready, n + 1)
                dve.reciprocal(stats[:, 3, :], stats[:, 2, :])
                dve.drain()
                for t in range(TILES):
                    last = dve.tensor_scalar(w2[:, t, :], w2[:, t, :], stats[:, 3, t:t + 1], None, ALU.mult)
                last.then_inc(prob_ready, 1)
                dve.wait_ge(turn_ready, n + 1)
                dve.scalar_tensor_tensor(w1[:, :, :], w2[:, :, :], TURNS, wi[:, :, :], ALU.mult,
                                         ALU.subtract).then_inc(frac_ready, 1)
                dve.wait_ge(wave_ready, n + 1)
                dve.tensor_tensor(w1[:, :, :], w1[:, :, :], sc[:, :, :], ALU.mult)
                dve.drain()
                dve.tensor_tensor(w1[:, :, :], w1[:, :, :], wi[:, :, :].bitcast(F32), ALU.add)
                dve.drain()
                dve.tensor_tensor(w1[:, :, :], w1[:, :, :], w2[:, :, :], ALU.mult).then_inc(weights_ready, 1)
                dve.drain()
                dve.tensor_tensor(pa[:, :, :].rearrange("p (t c) d -> p t c d", c=CAND),
                                  kv_c[:, :, DK:].rearrange("p (t c) d -> p t c d", c=CAND),
                                  w1[:, :, S:W].unsqueeze(3).broadcast_to([P, TILES, CAND, DK]), ALU.mult)
                dve.drain()
                dve.tensor_reduce(out_c[:, :, :], pa[:, :, :].rearrange("p (t c) d -> p t d c", c=CAND),
                                  AX.X, ALU.add)
                dve.drain()
                dve.wait_ge(pv_ready, n * TILES + TILES)
                dve.wait_ge(stored, n * 32)
                dve.tensor_tensor(out[:, :, :], ps[:, 7, 0:TILES * DK].rearrange("p (t d) -> p t d", d=DK),
                                  out_c[:, :, :], ALU.add).then_inc(out_ready, 1)


def experts(nc, a, s, out):
    with ExitStack() as ctx:
        def sb(name, shape, dt=F32):
            return ctx.enter_context(nc.sbuf_tensor("c_" + name, shape, dt))

        def sem(name):
            return ctx.enter_context(nc.semaphore("c_" + name))

        KB = LAT // P
        ident = sb("ident", [P, P])
        ones = sb("ones", [1, P])
        w_o = sb("w_o", [P, KB, D])
        w_r = sb("w_r", [D, EXPERTS])
        w_1 = sb("w_1", [D, EXPERTS, HID])
        w_2 = sb("w_2", [HID, EXPERTS, D])
        b_1 = sb("b_1", [HID, EXPERTS])
        b_2 = sb("b_2", [1, EXPERTS * D])
        vec = sb("vec", [P, 3, D])
        b_r = sb("b_r", [P, EXPERTS])
        slots = sb("slots", [P, EXPERTS])
        h = sb("h", [P, 2, D])
        heads = sb("heads", [P, 2, LAT])
        heads_t = sb("heads_t", [P, KB, P])
        res = sb("res", [P, D])
        x2 = sb("x2", [P, D])
        xn = sb("xn", [P, D])
        xn_t = sb("xn_t", [D, P])
        stats = sb("stats", [P, 6])
        agg = sb("agg", [P, 2])
        col = sb("col", [P, 8])
        logits = sb("logits", [P, EXPERTS])
        top = sb("top", [P, 8])
        top_i = sb("top_i", [P, 8], U32)
        top_f = sb("top_f", [P, 2])
        gate = sb("gate", [P, EXPERTS])
        gate2 = sb("gate2", [P, EXPERTS])
        hid = sb("hid", [HID, EXPERTS, P])
        mix = sb("mix", [P, EXPERTS, D])
        y = sb("y", [P, D])
        y_out = sb("y_out", [P, D])
        ps = ctx.enter_context(nc.psum_tensor("c_ps", [P, 8, 512], F32))
        ps_t, ps_o, ps_x, ps_r = ps[:, 0, :], ps[:, 1, 0:D], ps[0:D, 2, 0:P], ps[:, 3, 0:EXPERTS]
        ps_y = ps[:, 6, :]

        def ps_h(e):
            return ps[:, 4 + e // 4, P * (e % 4):P * (e % 4) + P]

        consts_in = sem("consts_in")
        ident_ready = sem("ident_ready")
        rows_in = [sem(f"rows_in{j}") for j in range(2)]
        heads_psum = sem("heads_psum")
        heads_ready = sem("heads_ready")
        proj_ready = sem("proj_ready")
        var_ready = sem("var_ready")
        root_ready = sem("root_ready")
        xn_ready = sem("xn_ready")
        xt_psum = sem("xt_psum")
        xt_ready = sem("xt_ready")
        logits_psum = sem("logits_psum")
        hid_psum = sem("hid_psum")
        hid_ready = sem("hid_ready")
        gap_ready = sem("gap_ready")
        odds_ready = sem("odds_ready")
        y_psum = sem("y_psum")
        y_ready = sem("y_ready")
        tiles_done = sem("tiles_done")
        stored = sem("stored")
        passed = sem("passed")

        block = ctx.enter_context(nc.Block())

        @block.sync
        def _(sp):
            for dst, src in ((w_o[:, :, :], a["Wo"].rearrange("(k p) d -> p k d", p=P)),
                             (w_r[:, :], a["Wr"]),
                             (w_1[:, :, :], a["W1"].rearrange("e d h -> d e h")),
                             (w_2[:, :, :], a["W2"].rearrange("e h d -> h e d")),
                             (b_1[:, :], a["b1_t"]),
                             (b_2[:, :], a["b2"].rearrange("(o e) d -> o (e d)", o=1)),
                             (vec[:, 0, :], a["bo"].partition_broadcast(P)),
                             (vec[:, 1, :], a["gamma"].partition_broadcast(P)),
                             (vec[:, 2, :], a["beta2"].partition_broadcast(P)),
                             (b_r[:, :], a["br"].partition_broadcast(P))):
                sp.dma_start(dst, src).then_inc(consts_in, 16)
            with sp.Fori(0, B) as b:
                with sp.Fori(0, TILES // 2) as tt:
                    for j in range(2):
                        n = b * TILES + tt * 2 + j
                        sp.wait_ge(y_ready, n + 1)
                        sp.dma_start(out[b, bass.ds((tt * 2 + j) * STRIDE, STRIDE), :],
                                     y_out[0:STRIDE, :]).then_inc(stored, 16)
                sp.dma_start(out[b, S - TAIL:S, :], y_out[STRIDE:P, :]).then_inc(stored, 16)
            sp.wait_ge(stored, B * 16 * (TILES + 1))

        @block.gpsimd
        def _(gp):
            gp.memset(ident[:, :], 0.0)
            gp.memset(ones[:, :], 1.0)
            gp.iota(slots[:, :], pattern=[[1, EXPERTS]], base=0, channel_multiplier=0,
                    allow_small_or_imprecise_dtypes=True).then_inc(ident_ready, 1)
            gp.wait_ge(ident_ready, 1)
            gp.affine_select(out=ident[:, :], in_=ident[:, :], compare_op=ALU.not_equal, fill=1.0,
                             base=0, pattern=[[-1, P]], channel_multiplier=1).then_inc(ident_ready, 1)
            with gp.Fori(0, B) as b:
                with gp.Fori(0, TILES // 2) as tt:
                    for j in range(2):
                        n = b * TILES + tt * 2 + j
                        row = (tt * 2 + j) * STRIDE
                        gp.wait_ge(tiles_done, n + 1)
                        gp.dma_start(h[:, j, :], s["h"][b, bass.ds(row, P), :]).then_inc(rows_in[j], 16)
                        gp.dma_start(heads[:, j, :], s["ctx"][b, bass.ds(row, P), :]).then_inc(rows_in[j], 16)

        @block.tensor
        def _(pe):
            pe.wait_ge(ident_ready, 2)
            pe.wait_ge(consts_in, 160)
            with pe.Fori(0, B * TILES // 2) as pair:
                for j in range(2):
                    n = pair * 2 + j
                    pe.wait_ge(rows_in[j], pair * 32 + 32)
                    for k in range(KB):
                        mm = pe.transpose(ps_t[:, P * k:P * k + P], heads[:, j, P * k:P * k + P], ident[:, :])
                    mm.then_inc(heads_psum, 1)
                    pe.wait_ge(heads_ready, n + 1)
                    for k in range(KB):
                        mm = pe.matmul(ps_o, heads_t[:, k, :], w_o[:, k, :], start=(k == 0), stop=(k == KB - 1))
                    mm.then_inc(proj_ready, 1)
                    wait_alone(pe, xn_ready, n + 1, passed)
                    pe.transpose(ps_x, xn[:, :], ident[:, :]).then_inc(xt_psum, 1)
                    pe.wait_ge(xt_ready, n + 1)
                    pe.matmul(ps_r, xn_t[:, :], w_r[:, :], start=True, stop=True).then_inc(logits_psum, 1)
                    for e in range(EXPERTS):
                        mm = pe.matmul(ps_h(e), w_1[:, e, :], xn_t[:, :], start=True, stop=True)
                        if e % 4 == 3:
                            mm.then_inc(hid_psum, 1)
                    pe.matmul(ps_y, ones[:, :], b_2[:, :], start=True, stop=False, skip_group_check=True)
                    for e in range(EXPERTS):
                        pe.wait_ge(hid_ready, n * EXPERTS + e + 1)
                        mm = pe.matmul(ps_y[:, D * e:D * e + D], hid[:, e, :], w_2[:, e, :],
                                       start=False, stop=(e == EXPERTS - 1), skip_group_check=True)
                    mm.then_inc(y_psum, 1)

        @block.scalar
        def _(act):
            act.wait_ge(consts_in, 160)
            with act.Fori(0, B * TILES) as n:
                act.wait_ge(heads_psum, n + 1)
                act.activation(heads_t[:, :, :].rearrange("p k n -> p (k n)"), ps_t, ACT.Copy).then_inc(heads_ready, 1)
                for i in range(2):
                    act.wait_ge(var_ready, n * 2 + i + 1)
                    act.activation(col[:, 1:2], col[:, 0:1], ACT.Sqrt).then_inc(root_ready, 1)
                act.wait_ge(xt_psum, n + 1)
                act.activation(xn_t[:, :], ps_x, ACT.Copy).then_inc(xt_ready, 1)
                for e in range(EXPERTS):
                    act.wait_ge(hid_psum, n * 2 + e // 4 + 1)
                    act.activation(hid[:, e, :], ps_h(e), ACT.Gelu, bias=b_1[:, e:e + 1]).then_inc(hid_ready, 1)
                act.wait_ge(gap_ready, n + 1)
                act.activation(col[:, 5:6], col[:, 4:5], ACT.Exp).then_inc(odds_ready, 1)

        @block.vector
        def _(dve):
            def c(i):
                return col[:, i:i + 1]

            def norm(dst, src, count):
                dve.bn_stats(stats[:, :], src)
                dve.drain()
                dve.bn_aggr(agg[:, :], stats[:, :])
                dve.drain()
                dve.tensor_scalar(c(0), agg[:, 1:2], LN_EPS, None, ALU.add).then_inc(var_ready, 1)
                dve.wait_ge(root_ready, count)
                dve.reciprocal(c(2), c(1))
                dve.drain()
                dve.tensor_tensor(c(2), c(2), c(0), ALU.mult)
                dve.drain()
                dve.tensor_tensor(c(2), c(2), c(1), ALU.add)
                dve.drain()
                dve.tensor_scalar(c(2), c(2), 0.5, None, ALU.mult)
                dve.drain()
                dve.reciprocal(c(3), c(2))
                dve.drain()
                dve.tensor_scalar(dst, src, agg[:, 0:1], c(3), ALU.subtract, ALU.mult)
                dve.drain()

            dve.wait_ge(ident_ready, 2)
            dve.wait_ge(consts_in, 160)
            dve.sem_inc(tiles_done, 2)
            with dve.Fori(0, B) as b:
                with dve.Fori(0, TILES // 2) as tt:
                    for j in range(2):
                        n = b * TILES + tt * 2 + j
                        dve.wait_ge(proj_ready, n + 1)
                        dve.tensor_tensor(res[:, :], ps_o, vec[:, 0, :], ALU.add)
                        dve.drain()
                        dve.wait_ge(rows_in[j], (b * (TILES // 2) + tt) * 32 + 32)
                        dve.tensor_tensor(res[:, :], res[:, :], h[:, j, :], ALU.add).then_inc(tiles_done, 1)
                        dve.drain()
                        norm(x2[:, :], res[:, :], n * 2 + 1)
                        norm(xn[:, :], x2[:, :], n * 2 + 2)
                        dve.tensor_tensor(xn[:, :], xn[:, :], vec[:, 1, :], ALU.mult)
                        dve.drain()
                        dve.tensor_tensor(xn[:, :], xn[:, :], vec[:, 2, :], ALU.add).then_inc(xn_ready, 1)
                        dve.wait_ge(logits_psum, n + 1)
                        dve.tensor_tensor(logits[:, :], ps_r, b_r[:, :], ALU.add)
                        dve.drain()
                        dve.max(top[:, :], logits[:, :])
                        dve.drain()
                        dve.max_index(top_i[:, :], top[:, :], logits[:, :])
                        dve.tensor_tensor(c(4), top[:, 1:2], top[:, 0:1], ALU.subtract).then_inc(gap_ready, 1)
                        dve.drain()
                        dve.tensor_copy(top_f[:, :], top_i[:, 0:2])
                        dve.wait_ge(odds_ready, n + 1)
                        dve.tensor_scalar(c(6), c(5), 1.0, None, ALU.add)
                        dve.drain()
                        dve.reciprocal(c(6), c(6))
                        dve.drain()
                        dve.tensor_tensor(c(7), c(5), c(6), ALU.mult)
                        dve.drain()
                        dve.tensor_scalar(gate[:, :], slots[:, :], top_f[:, 0:1], c(6), ALU.is_equal, ALU.mult)
                        dve.tensor_scalar(gate2[:, :], slots[:, :], top_f[:, 1:2], c(7), ALU.is_equal, ALU.mult)
                        dve.drain()
                        dve.tensor_tensor(gate[:, :], gate[:, :], gate2[:, :], ALU.add)
                        dve.drain()
                        dve.wait_ge(y_psum, n + 1)
                        dve.tensor_tensor(mix[:, :, :], ps_y.rearrange("p (e d) -> p e d", e=EXPERTS),
                                          gate[:, :].unsqueeze(2).broadcast_to([P, EXPERTS, D]), ALU.mult)
                        dve.drain()
                        dve.tensor_reduce(y[:, :], mix[:, :, :].rearrange("p e d -> p d e"), AX.X, ALU.add)
                        dve.drain()
                        dve.wait_ge(stored, b * (TILES + 1) * 16 + (tt * 2 + j) * 16)
                        dve.tensor_tensor(y_out[:, :], y[:, :], res[:, :], ALU.add).then_inc(y_ready, 1)
                        dve.drain()


def build(nc, a, out):
    s = {"h": nc.dram_tensor("h", (B, S, D), F32, kind="Internal").ap(),
         "q": nc.dram_tensor("q", (B, HEADS, S, DK), F32, kind="Internal").ap(),
         "kv": nc.dram_tensor("kv", (B, HEADS, S, 2 * DK), F32, kind="Internal").ap(),
         "ctx": nc.dram_tensor("ctx", (B, S, LAT), F32, kind="Internal").ap()}
    tokens_and_projections(nc, a, s)
    attention(nc, s)
    experts(nc, a, s, out)


def kernel(x, L0_tok_kernel, L0_tok_bias, L0_tok_beta, L0_tok_moving_mean, L0_tok_moving_var,
           L0_attn_Wq, L0_attn_bq, L0_attn_Wk, L0_attn_bk, L0_attn_Wv, L0_attn_bv, L0_attn_Wo, L0_attn_bo,
           L0_ffn_gamma, L0_ffn_beta, L0_ffn_Wr, L0_ffn_br, L0_ffn_W1, L0_ffn_b1, L0_ffn_W2, L0_ffn_b2):
    from concourse import bacc
    from concourse.bass_utils import run_bass_kernel_spmd

    x_t = np.asarray(x).transpose(0, 2, 1)
    x_tiles = np.stack([x_t[b, :, STRIDE * t:STRIDE * t + P + TAPS - 1] for b in range(B) for t in range(TILES)])
    arrays = {
        "x_tiles": x_tiles, "kernel": L0_tok_kernel, "bias": L0_tok_bias, "beta": L0_tok_beta,
        "moving_mean": L0_tok_moving_mean, "moving_var": L0_tok_moving_var,
        "Wq": L0_attn_Wq, "bq": L0_attn_bq, "Wk": L0_attn_Wk, "bk": L0_attn_bk, "Wv": L0_attn_Wv,
        "bv": L0_attn_bv, "Wo": L0_attn_Wo, "bo": L0_attn_bo, "gamma": L0_ffn_gamma, "beta2": L0_ffn_beta,
        "Wr": L0_ffn_Wr, "br": L0_ffn_br, "W1": L0_ffn_W1, "b1_t": np.asarray(L0_ffn_b1).T,
        "W2": L0_ffn_W2, "b2": L0_ffn_b2,
    }
    arrays = {name: np.ascontiguousarray(v) for name, v in arrays.items()}
    nc = bacc.Bacc("TRN2", target_bir_lowering=False, num_devices=1)
    a = {name: nc.dram_tensor("in_" + name, v.shape, mybir.dt.from_np(v.dtype), kind="ExternalInput").ap()
         for name, v in arrays.items()}
    out = nc.dram_tensor("out", (B, S, D), F32, kind="ExternalOutput").ap()
    build(nc, a, out)
    got = run_bass_kernel_spmd(nc, [{"in_" + name: v for name, v in arrays.items()}], core_ids=[0])
    return got.results[0]["out"]
```

```python
import math
from contextlib import ExitStack

import numpy as np

import concourse.bass as bass
from concourse import mybir

F32 = mybir.dt.float32
BF16 = mybir.dt.bfloat16
F32R = mybir.dt.float32r
I32 = mybir.dt.int32
U32 = mybir.dt.uint32
ALU = mybir.AluOpType
ACT = mybir.ActivationFunctionType
AX = mybir.AxisListType

B = 8
S_IN = 750
TAPS = 3
S = S_IN - TAPS + 1
C_IN = 128
D = 64
HEADS = 8
DK = 64
LAT = HEADS * DK
P = 128
TILES = -(-S // P)
STRIDE = (S - P) // (TILES - 1)
assert STRIDE * (TILES - 1) + P == S
TAIL = P - STRIDE
EXPERTS = 8
HID = 128
CAND = 8
HIGH_BITS = ~0xFFF
M_PROJ = 1.5 * 2.0 ** 6
M_SCORE = 1.5 * 2.0 ** 11
BN_EPS = 1e-3
LN_EPS = 1e-5


def wait_alone(engine, semaphore, value, passed):
    engine.wait_ge(semaphore, value)
    engine.sem_inc(passed, 1)


def tokens_and_projections(nc, a, s):
    with ExitStack() as ctx:
        def sb(name, shape, dt=F32):
            return ctx.enter_context(nc.sbuf_tensor("a_" + name, shape, dt))

        def sem(name):
            return ctx.enter_context(nc.semaphore("a_" + name))

        x_t = sb("x_t", [C_IN, TILES, P + TAPS - 1])
        x_sign = sb("x_sign", [C_IN, TILES, P + TAPS - 1], BF16)
        k_raw = sb("k_raw", [C_IN, TAPS, D])
        k_sign = sb("k_sign", [C_IN, TAPS, D], BF16)
        w_qk = sb("w_qk", [P, 2 * LAT])
        w_tmp = sb("w_tmp", [P, 2, 2 * LAT])
        w_hh = sb("w_hh", [P, 2 * LAT], F32R)
        w_cross = sb("w_cross", [P, 2 * LAT], F32R)
        w_ll = sb("w_ll", [P, 2 * LAT], F32R)
        unit = sb("unit", [P, P], F32R)
        neg_unit = sb("neg_unit", [P, P], F32R)
        m_left = sb("m_left", [P, P], BF16)
        m_right = sb("m_right", [P, 512], BF16)
        w_v = sb("w_v", [P, LAT])
        b_qk = sb("b_qk", [P, 2 * LAT])
        b_v = sb("b_v", [P, LAT])
        vec = sb("vec", [P, 3, D])
        ident = sb("ident", [P, P])
        row_mask = sb("row_mask", [P, D + 2])
        m_col = sb("m_col", [P, 2])
        ones = sb("ones", [P, P])
        var_col = sb("var_col", [D, 12])
        inv = sb("inv", [P, D])
        inv_diag = sb("inv_diag", [D, D])
        h = sb("h", [P, TILES, D])
        red = sb("red", [P, TILES, 64])
        col = sb("col", [P, 8, TILES])
        dev = sb("dev", [P, TILES, D])
        sq = sb("sq", [P, TILES, D])
        q0 = sb("q0", [P, TILES, D])
        q_hi = sb("q_hi", [P, TILES, D])
        q_lo = sb("q_lo", [P, TILES, D])
        z_cat = sb("z_cat", [P, TILES, 2, D])
        z_t = sb("z_t", [P, TILES, P])
        z_row = sb("z_row", [P, 2, P], F32R)
        coarse_a = sb("coarse_a", [P, 2, 2 * LAT], F32R)
        grid_acc = sb("grid_acc", [P, 2, 2 * LAT])
        rest = sb("rest", [P, 2, 2 * LAT], F32R)
        high = sb("high", [P, 2, 2 * LAT])
        acc = sb("acc", [P, 2, 2 * LAT])
        qk = sb("qk", [P, 2, 2 * LAT])
        v = sb("v", [P, TILES, LAT])
        ps = ctx.enter_context(nc.psum_tensor("a_ps", [P, 8, 512], F32))
        ps_conv = ps[:, 0, 0:TILES * D].rearrange("p (t d) -> p t d", d=D)

        def ps_zt(t):
            return ps[:, 1 + t // 4, P * (t % 4):P * (t % 4) + P]

        def ps_v(t):
            return ps[:, (3 + t) % 8, :]

        ps_inv = ps[:, 3, 0:D]

        def prod_a(x):
            return ps[:, 4 * x:4 * x + 2, :]

        def low(x):
            return ps[:, 4 * x + 2:4 * x + 4, :]

        def banked(t):
            return t.rearrange("p (a n) -> p a n", a=2)

        consts_in = sem("consts_in")
        x_in = sem("x_in")
        ident_ready = sem("ident_ready")
        w_split = sem("w_split")
        rs_dve = sem("rs_dve")
        rs_act = sem("rs_act")
        diag_ready = sem("diag_ready")
        inv_ready = sem("inv_ready")
        sign_ready = sem("sign_ready")
        conv_ready = sem("conv_ready")
        var_ready = sem("var_ready")
        root_ready = sem("root_ready")
        z_ready = sem("z_ready")
        zt_psum = sem("zt_psum")
        zt_ready = sem("zt_ready")
        v_psum = sem("v_psum")
        v_ready = sem("v_ready")

        def pair_sems(name):
            return [sem(f"{name}{x}") for x in range(2)]

        row_ready = pair_sems("row_ready")
        prod_ready = pair_sems("prod_ready")
        coarse_ready = pair_sems("coarse_ready")
        low_ready = pair_sems("low_ready")
        rest_ready = pair_sems("rest_ready")
        high_ready = pair_sems("high_ready")
        t_ready = pair_sems("t_ready")
        acc_ready = pair_sems("acc_ready")
        gacc_ready = pair_sems("gacc_ready")
        out_free = sem("out_free")
        rows_free = sem("rows_free")
        qk_ready = sem("qk_ready")
        stored = sem("stored")
        passed = sem("passed")
        rows_stored = sem("rows_stored")

        block = ctx.enter_context(nc.Block())

        @block.sync
        def _(sp):
            for dst, src in ((k_raw[:, :, :], a["kernel"].rearrange("w c d -> c w d")),
                             (w_qk[0:D, 0:LAT], a["Wq"]), (w_qk[D:P, 0:LAT], a["Wq"]),
                             (w_qk[0:D, LAT:], a["Wk"]), (w_qk[D:P, LAT:], a["Wk"]),
                             (w_v[0:D, :], a["Wv"]), (w_v[D:P, :], a["Wv"]),
                             (b_qk[:, 0:LAT], a["bq"].partition_broadcast(P)),
                             (b_qk[:, LAT:], a["bk"].partition_broadcast(P)),
                             (b_v[:, :], a["bv"].partition_broadcast(P)),
                             (vec[:, 0, :], a["bias"].partition_broadcast(P)),
                             (vec[:, 1, :], a["moving_mean"].partition_broadcast(P)),
                             (vec[:, 2, :], a["beta"].partition_broadcast(P)),
                             (var_col[:, 0:1], a["moving_var"].rearrange("(d o) -> d o", o=1))):
                sp.dma_start(dst, src).then_inc(consts_in, 16)
            sp.sem_inc(rows_free, 1)
            sp.sem_inc(out_free, 2)

            def by_head(dst, src):
                return dst.rearrange("h r d -> r h d"), src.rearrange("r (h d) -> r h d", h=HEADS)

            def store_qk(b, n, x, row, rows):
                sp.wait_ge(qk_ready, n + 1)
                at = bass.ds(row, rows)
                sp.dma_start(*by_head(s["q"][b, :, at, :], qk[0:rows, x, 0:LAT])).then_inc(stored, 16)
                sp.dma_start(*by_head(s["kv"][b, :, at, 0:DK], qk[0:rows, x, LAT:])).then_inc(stored, 16)
                sp.wait_ge(stored, (n + 1) * 32)
                sp.sem_inc(out_free, 1)

            with sp.Fori(0, B) as b:
                sp.wait_ge(v_ready, b + 1)
                for t in range(TILES):
                    rows = P if t == TILES - 1 else STRIDE
                    at = slice(t * STRIDE, t * STRIDE + rows)
                    sp.dma_start(s["h"][b, at, :], h[0:rows, t, :]).then_inc(rows_stored, 16)
                    sp.dma_start(*by_head(s["kv"][b, :, at, DK:], v[0:rows, t, :])).then_inc(rows_stored, 16)
                sp.wait_ge(rows_stored, (b + 1) * (TILES * 32))
                sp.sem_inc(rows_free, 1)
                with sp.Fori(0, TILES // 2 - 1) as tt:
                    for x in range(2):
                        store_qk(b, b * TILES + tt * 2 + x, x, (tt * 2 + x) * STRIDE, STRIDE)
                store_qk(b, b * TILES + TILES - 2, 0, (TILES - 2) * STRIDE, STRIDE)
                store_qk(b, b * TILES + TILES - 1, 1, S - P, P)

        @block.gpsimd
        def _(gp):
            gp.memset(ident[:, :], 0.0)
            gp.memset(row_mask[:, :], 0.0)
            gp.memset(ones[:, :], 1.0)
            gp.memset(m_left[:, :], 0.0)
            gp.memset(m_right[:, :], 0.0)
            gp.drain()
            gp.memset(m_left[0:1, :], 1.0)
            gp.memset(m_right[0:1, :], M_PROJ)
            gp.memset(m_col[:, 0:1], M_PROJ)
            gp.memset(m_col[:, 1:2], -M_PROJ).then_inc(ident_ready, 1)
            gp.wait_ge(ident_ready, 1)
            gp.affine_select(out=ident[:, :], in_=ident[:, :], compare_op=ALU.not_equal, fill=1.0,
                             base=0, pattern=[[-1, P]], channel_multiplier=1)
            gp.affine_select(out=row_mask[:, :], in_=row_mask[:, :], compare_op=ALU.not_equal, fill=1.0,
                             base=0, pattern=[[-1, D + 2]], channel_multiplier=1).then_inc(ident_ready, 1)
            gp.wait_ge(ident_ready, 2)
            gp.affine_select(out=row_mask[:, :], in_=row_mask[:, :], compare_op=ALU.not_equal, fill=1.0,
                             base=-D, pattern=[[-1, D + 2]], channel_multiplier=1).then_inc(ident_ready, 1)
            x_of = a["x_tiles"].rearrange("(b t) c r -> b c t r", t=TILES)
            gp.dma_start(x_t[:, :, :], x_of[0, :, :, :]).then_inc(x_in, 16)
            with gp.Fori(0, B - 1) as b:
                gp.wait_ge(sign_ready, b + 1)
                gp.dma_start(x_t[:, :, :], x_of[bass.ds(b + 1, 1), :, :, :]
                             .rearrange("o c t r -> (o c) t r")).then_inc(x_in, 16)

        def rows_of_batch(dve, b):
            def c(i):
                return col[:, i, :]

            def each(x):
                return x.unsqueeze(2).broadcast_to([P, TILES, D])

            def all_tiles(x):
                return x.unsqueeze(1).broadcast_to([P, TILES, D])

            def split(hi, lo, x):
                dve.tensor_scalar(hi.bitcast(I32), x.bitcast(I32), HIGH_BITS, None, ALU.bitwise_and)
                dve.drain()
                dve.tensor_tensor(lo, x, hi, ALU.subtract)
                dve.drain()

            dve.wait_ge(x_in, b * 16 + 16)
            dve.tensor_scalar(x_sign[:, :, :], x_t[:, :, :], 0.0, 0.5, ALU.is_ge,
                              ALU.subtract).then_inc(sign_ready, 1)
            dve.wait_ge(rows_free, b + 1)
            dve.wait_ge(conv_ready, b + 1)
            dve.scalar_tensor_tensor(h[:, :, :], ps_conv, 4.0, all_tiles(vec[:, 0, :]), ALU.mult, ALU.add)
            dve.drain()
            dve.tensor_tensor(h[:, :, :], h[:, :, :], all_tiles(vec[:, 1, :]), ALU.subtract)
            dve.drain()
            dve.tensor_tensor(h[:, :, :], h[:, :, :], all_tiles(inv[:, :]), ALU.mult)
            dve.drain()
            dve.tensor_tensor(h[:, :, :], h[:, :, :], all_tiles(vec[:, 2, :]), ALU.add)
            dve.drain()
            dve.tensor_tensor(red[:, :, 0:16], h[:, :, 0:16], h[:, :, 16:32], ALU.add)
            dve.drain()
            dve.tensor_tensor(red[:, :, 0:16], red[:, :, 0:16], h[:, :, 32:48], ALU.add)
            dve.drain()
            dve.tensor_tensor(red[:, :, 0:16], red[:, :, 0:16], h[:, :, 48:64], ALU.add)
            dve.drain()
            for i in range(2):
                dve.tensor_tensor(red[:, :, 16 + 4 * i:20 + 4 * i], red[:, :, 8 * i:8 * i + 4],
                                  red[:, :, 8 * i + 4:8 * i + 8], ALU.add)
            dve.drain()
            dve.tensor_tensor(red[:, :, 24:28], red[:, :, 16:20], red[:, :, 20:24], ALU.add)
            dve.drain()
            dve.tensor_tensor(red[:, :, 28:30], red[:, :, 24:28:2], red[:, :, 25:28:2], ALU.add)
            dve.drain()
            dve.tensor_tensor(c(0), red[:, :, 28], red[:, :, 29], ALU.add)
            dve.drain()
            dve.tensor_scalar(c(0), c(0), 1.0 / D, None, ALU.mult)
            dve.drain()
            dve.tensor_tensor(dev[:, :, :], h[:, :, :], each(c(0)), ALU.subtract)
            dve.drain()
            dve.tensor_tensor(sq[:, :, :], dev[:, :, :], dev[:, :, :], ALU.mult)
            dve.drain()
            dve.tensor_reduce(red[:, :, 32:34], sq[:, :, :].rearrange("p t (a n) -> p t a n", a=2), AX.X, ALU.add)
            dve.drain()
            dve.tensor_tensor(c(1), red[:, :, 32], red[:, :, 33], ALU.add)
            dve.drain()
            dve.tensor_scalar(c(1), c(1), 1.0 / D, LN_EPS, ALU.mult, ALU.add).then_inc(var_ready, 1)
            dve.wait_ge(root_ready, b + 1)
            dve.reciprocal(c(3), c(2))
            split(c(4), c(5), c(2))
            dve.tensor_tensor(c(6), c(4), c(4), ALU.mult)
            dve.drain()
            dve.tensor_tensor(c(6), c(1), c(6), ALU.subtract)
            dve.tensor_tensor(c(7), c(4), c(5), ALU.mult)
            dve.drain()
            dve.scalar_tensor_tensor(c(6), c(7), -2.0, c(6), ALU.mult, ALU.add)
            dve.drain()
            dve.tensor_tensor(c(7), c(5), c(5), ALU.mult)
            dve.drain()
            dve.tensor_tensor(c(6), c(6), c(7), ALU.subtract)
            dve.drain()
            dve.scalar_tensor_tensor(c(6), c(6), 0.5, c(3), ALU.mult, ALU.mult)
            dve.drain()
            dve.tensor_tensor(c(2), c(2), c(6), ALU.add)
            dve.drain()
            dve.reciprocal(c(3), c(2))
            split(c(4), c(5), c(2))
            dve.tensor_tensor(q0[:, :, :], dev[:, :, :], each(c(3)), ALU.mult)
            dve.drain()
            split(q_hi[:, :, :], q_lo[:, :, :], q0[:, :, :])
            dve.tensor_scalar(c(6), c(4), -1.0, None, ALU.mult)
            dve.tensor_scalar(c(7), c(5), -1.0, None, ALU.mult)
            dve.drain()
            for part, factor in ((q_hi, c(6)), (q_hi, c(7)), (q_lo, c(6)), (q_lo, c(7))):
                dve.tensor_tensor(sq[:, :, :], part[:, :, :], each(factor), ALU.mult)
                dve.drain()
                dve.tensor_tensor(dev[:, :, :], sq[:, :, :], dev[:, :, :], ALU.add)
                dve.drain()
            dve.tensor_tensor(dev[:, :, :], dev[:, :, :], each(c(3)), ALU.mult)
            dve.drain()
            dve.tensor_tensor(q0[:, :, :], dev[:, :, :], q0[:, :, :], ALU.add)
            dve.drain()
            dve.tensor_scalar(z_cat[:, :, 0, :].bitcast(I32), q0[:, :, :].bitcast(I32), HIGH_BITS, None,
                              ALU.bitwise_and)
            dve.drain()
            dve.tensor_tensor(z_cat[:, :, 1, :], q0[:, :, :], z_cat[:, :, 0, :], ALU.subtract).then_inc(z_ready, 1)
            dve.wait_ge(v_psum, b + 1)
            for t in range(TILES):
                last = dve.tensor_tensor(v[:, t, :], ps_v(t), b_v[:, :], ALU.add)
            last.then_inc(v_ready, 1)

        @block.vector
        def _(dve):
            def split(hi, lo, x):
                dve.tensor_scalar(hi.bitcast(I32), x.bitcast(I32), HIGH_BITS, None, ALU.bitwise_and)
                dve.drain()
                dve.tensor_tensor(lo, x, hi, ALU.subtract)
                dve.drain()

            dve.wait_ge(consts_in, 14 * 16)
            dve.tensor_scalar(k_sign[:, :, :], k_raw[:, :, :], 0.0, 0.5, ALU.is_ge, ALU.subtract)
            split(w_tmp[:, 0, :], w_tmp[:, 1, :], w_qk[:, :])
            dve.memset(w_hh[D:P, :].bitcast(F32), 0.0)
            dve.memset(w_ll[0:D, :].bitcast(F32), 0.0)
            dve.tensor_copy(w_hh[0:D, :], w_tmp[0:D, 0, :])
            dve.tensor_copy(w_cross[0:D, :], w_tmp[0:D, 1, :])
            dve.tensor_copy(w_cross[D:P, :], w_tmp[D:P, 0, :])
            dve.tensor_copy(w_ll[D:P, :], w_tmp[D:P, 1, :])

            def c(n):
                return var_col[:, n:n + 1]
            dve.tensor_scalar(c(1), c(0), BN_EPS, None, ALU.add)
            dve.drain()
            dve.tensor_scalar(c(2).bitcast(I32), c(1).bitcast(I32), ~0x1FFF, 0x1000, ALU.bitwise_and,
                              ALU.bitwise_or).then_inc(rs_dve, 1)
            dve.wait_ge(rs_act, 1)
            dve.reciprocal(c(4), c(3))
            dve.drain()
            for _ in range(2):
                dve.tensor_tensor(c(5), c(4), c(4), ALU.mult)
                dve.drain()
                dve.tensor_tensor(c(5), c(5), c(2), ALU.mult)
                dve.drain()
                dve.tensor_scalar(c(5), c(5), -0.5, 1.5, ALU.mult, ALU.add)
                dve.drain()
                dve.tensor_tensor(c(4), c(4), c(5), ALU.mult)
                dve.drain()
            dve.tensor_scalar(c(5), c(4), 2.0 ** 11 + 1, None, ALU.mult)
            dve.drain()
            dve.tensor_tensor(c(6), c(5), c(4), ALU.subtract)
            dve.drain()
            dve.tensor_tensor(c(6), c(5), c(6), ALU.subtract)
            dve.drain()
            for i in range(2):
                dve.tensor_tensor(c(7), c(1), c(6), ALU.mult)
                dve.tensor_scalar(c(8), c(6), -0.5, None, ALU.mult).then_inc(rs_dve, 1)
                dve.wait_ge(rs_act, 2 + i)
                dve.tensor_copy(c(6), c(10))
                dve.drain()
            dve.wait_ge(ident_ready, 3)
            dve.tensor_copy(unit[:, :], ident[:, :])
            dve.tensor_scalar(neg_unit[:, :], ident[:, :], -1.0, None, ALU.mult)
            dve.tensor_scalar(inv_diag[:, :], ident[0:D, 0:D], c(6), None, ALU.mult).then_inc(diag_ready, 1)
            dve.wait_ge(inv_ready, 1)
            dve.tensor_copy(inv[:, :], ps_inv).then_inc(w_split, 1)

            for x in range(2):
                dve.memset(acc[:, x, :], 0.0).then_inc(acc_ready[x], 1)
            with dve.Fori(0, B) as b:
                rows_of_batch(dve, b)
                with dve.Fori(0, TILES // 2) as tt:
                    m = b * (TILES // 2) + tt

                    def acc_rest(k, x):
                        dve.wait_ge(gacc_ready[x], m * D + k + 1)
                        dve.scalar_tensor_tensor(rest[:, x, :], grid_acc[:, x, :], M_PROJ, acc[:, x, :],
                                                 ALU.subtract, ALU.subtract,
                                                 reverse1=True).then_inc(rest_ready[x], 1)

                    def high_part(k, x):
                        dve.wait_ge(coarse_ready[x], m * D + k + 1)
                        dve.tensor_tensor(high[:, x, :], coarse_a[:, x, :].bitcast(F32), grid_acc[:, x, :],
                                          ALU.add).then_inc(high_ready[x], 1)

                    def new_acc(k, x):
                        dve.wait_ge(high_ready[x], m * D + k + 1)
                        dve.wait_ge(t_ready[x], m * D + k + 1)
                        dve.scalar_tensor_tensor(banked(acc[:, x, :]), banked(high[:, x, :]), M_PROJ, low(x),
                                                 ALU.subtract, ALU.add).then_inc(acc_ready[x], 1)

                    def finish(x):
                        dve.drain()
                        dve.wait_ge(out_free, m * 2 + x + 1)
                        dve.tensor_tensor(qk[:, x, :], acc[:, x, :], b_qk[:, :], ALU.add).then_inc(qk_ready, 1)
                        dve.drain()
                        dve.memset(acc[:, x, :], 0.0).then_inc(acc_ready[x], 1)

                    def step(k, last=False):
                        new_acc(k, 0)
                        acc_rest(k, 1)
                        high_part(k, 1)
                        if last:
                            finish(0)
                        else:
                            acc_rest(k + 1, 0)
                            high_part(k + 1, 0)
                        new_acc(k, 1)

                    acc_rest(0, 0)
                    high_part(0, 0)
                    with dve.Fori(0, D // 2 - 1) as kk:
                        step(kk * 2)
                        step(kk * 2 + 1)
                    step(D - 2)
                    step(D - 1, last=True)
                    finish(1)

        @block.scalar
        def _(act):
            def c(n):
                return var_col[:, n:n + 1]
            act.wait_ge(rs_dve, 1)
            act.activation(c(3), c(2), ACT.Sqrt).then_inc(rs_act, 1)
            act.wait_ge(ident_ready, 3)
            act.mul(c(11), ones[0:D, 0:1], -1.0)
            act.drain()
            for i in range(2):
                act.wait_ge(rs_dve, 2 + i)
                act.activation(c(9), c(7), ACT.Identity, bias=c(11), scale=c(6))
                act.drain()
                act.activation(c(10), c(9), ACT.Identity, bias=c(6), scale=c(8)).then_inc(rs_act, 1)
            with act.Fori(0, B) as b:
                act.wait_ge(var_ready, b + 1)
                act.activation(col[:, 2, :], col[:, 1, :], ACT.Sqrt).then_inc(root_ready, 1)
                act.wait_ge(zt_psum, b + 1)
                act.activation(z_t[:, 0:4, :].rearrange("p t n -> p (t n)"), ps[:, 1, :], ACT.Copy)
                act.activation(z_t[:, 4:TILES, :].rearrange("p t n -> p (t n)"), ps[:, 2, 0:P * (TILES - 4)],
                               ACT.Copy).then_inc(zt_ready, 1)
                act.drain()
                with act.Fori(0, TILES // 2) as tt:
                    m = b * (TILES // 2) + tt

                    def acc_grid(k, x):
                        act.wait_ge(acc_ready[x], m * (D + 1) + k + 1)
                        act.activation(grid_acc[:, x, :], acc[:, x, :], ACT.Identity,
                                       bias=m_col[:, 0:1]).then_inc(gacc_ready[x], 1)

                    def row(k, x, after=True):
                        if after:
                            wait_alone(act, low_ready[x], m * D + k, passed)
                        tile_t = z_t[:, bass.ds(tt * 2 + x, 1), :].rearrange("p t n -> p (t n)")
                        act.activation(z_row[:, x, :], tile_t, ACT.Copy,
                                       scale=row_mask[:, bass.ds(k, 1)]).then_inc(row_ready[x], 1)

                    def coarse(k, x, after=True):
                        if after:
                            act.wait_ge(high_ready[x], m * D + k)
                        act.wait_ge(prod_ready[x], m * D + k + 1)
                        act.activation(banked(coarse_a[:, x, :]), prod_a(x), ACT.Identity,
                                       bias=m_col[:, 1:2]).then_inc(coarse_ready[x], 1)

                    def step(k, last=False):
                        acc_grid(k + 1, 0)
                        row(k + 1, 1)
                        if not last:
                            row(k + 2, 0)
                        coarse(k + 1, 1)
                        if not last:
                            coarse(k + 2, 0)
                        acc_grid(k + 1, 1)

                    for x in range(2):
                        acc_grid(0, x)
                        row(0, x, after=False)
                    for x in range(2):
                        coarse(0, x, after=False)
                    row(1, 0)
                    coarse(1, 0)
                    with act.Fori(0, D // 2 - 1) as kk:
                        step(kk * 2)
                        step(kk * 2 + 1)
                    step(D - 2, last=True)

        @block.tensor
        def _(pe):
            pe.wait_ge(diag_ready, 1)
            pe.matmul(ps_inv, ones[0:D, :], inv_diag[:, :], start=True, stop=True).then_inc(inv_ready, 1)
            pe.wait_ge(w_split, 1)
            with pe.Fori(0, B) as b:
                pe.wait_ge(sign_ready, b + 1)
                for t in range(TILES):
                    for w in range(TAPS):
                        mm = pe.matmul(ps_conv[:, t, :], x_sign[:, t, w:w + P], k_sign[:, w, :],
                                       start=(w == 0), stop=(w == TAPS - 1))
                mm.then_inc(conv_ready, 1)
                wait_alone(pe, z_ready, b + 1, passed)
                for t in range(TILES):
                    mm = pe.transpose(ps_zt(t), z_cat[:, t, :, :].rearrange("p a d -> p (a d)"), ident[:, :])
                mm.then_inc(zt_psum, 1)
                pe.wait_ge(zt_ready, b + 1)
                for t in range(TILES):
                    mm = pe.matmul(ps_v(t), z_t[:, t, :], w_v[:, :], start=True, stop=True)
                mm.then_inc(v_psum, 1)
                wait_alone(pe, v_ready, b + 1, passed)
                with pe.Fori(0, TILES // 2) as tt:
                    m = b * (TILES // 2) + tt

                    def product(k, x):
                        pe.wait_ge(row_ready[x], m * D + k + 1)
                        for half in range(2):
                            dst = prod_a(x)[:, half, :]
                            pe.matmul(dst, m_left[:, :], m_right[:, :], start=True, stop=False)
                            mm = pe.matmul(dst, z_row[:, x, :], w_hh[:, 512 * half:512 * half + 512],
                                           start=False, stop=True)
                        mm.then_inc(prod_ready[x], 1)

                    def low_products(k, x):
                        pe.wait_ge(coarse_ready[x], m * D + k + 1)
                        pe.wait_ge(acc_ready[x], m * (D + 1) + k + 1)
                        for half in range(2):
                            at = slice(512 * half, 512 * half + 512)
                            dst = low(x)[:, half, :]
                            pe.matmul(dst, neg_unit[:, :], coarse_a[:, x, at], start=True, stop=False)
                            for w in (w_hh, w_cross, w_ll):
                                mm = pe.matmul(dst, z_row[:, x, :], w[:, at], start=False, stop=False)
                        mm.then_inc(low_ready[x], 1)

                    def add_rest(k, x):
                        pe.wait_ge(rest_ready[x], m * D + k + 1)
                        for half in range(2):
                            mm = pe.matmul(low(x)[:, half, :], unit[:, :], rest[:, x, 512 * half:512 * half + 512],
                                           start=False, stop=True)
                        mm.then_inc(t_ready[x], 1)

                    def step(k, last=False):
                        low_products(k + 1, 0)
                        add_rest(k, 1)
                        product(k + 1, 1)
                        if not last:
                            product(k + 2, 0)
                        add_rest(k + 1, 0)
                        low_products(k + 1, 1)

                    product(0, 0)
                    product(0, 1)
                    low_products(0, 0)
                    product(1, 0)
                    add_rest(0, 0)
                    low_products(0, 1)
                    with pe.Fori(0, D // 2 - 1) as kk:
                        step(kk * 2)
                        step(kk * 2 + 1)
                    step(D - 2, last=True)
                    add_rest(D - 1, 1)


def attention(nc, s):
    PHI = (1.0 + math.sqrt(5.0)) / 2.0
    PHI_INV = float(np.float32(1.0 / PHI))
    TURNS = PHI * math.sqrt(2.0) * 51.85 / (2.0 * math.pi)
    COS = math.pi / PHI
    TWO_PI = float(np.nextafter(np.float32(2.0 * math.pi), np.float32(0)))
    N = B * HEADS
    assert CAND == 8
    W = S + CAND
    HALF = S // 2
    NEG = -1e9
    TH = TILES // 2
    PC = TILES * CAND
    SMALL_OPS = 10 * (DK // 4 - 1)
    TURN_GROUPS = 2 * TILES
    assert N % 2 == 0 and N >= 4
    with ExitStack() as ctx:
        def sb(name, shape, dt=F32):
            return ctx.enter_context(nc.sbuf_tensor("b_" + name, shape, dt))

        def sem(name):
            return ctx.enter_context(nc.semaphore("b_" + name))

        ident = sb("ident", [P, P])
        q = sb("q", [P, 2, TILES, DK])
        kv = sb("kv", [P, 2, TILES, 2 * DK])
        sc = sb("sc", [P, 2, TILES, W])
        kv_c = sb("kv_c", [P, 2, PC, 2 * DK])
        q_hi = sb("q_hi", [P, TILES, DK])
        q_lo = sb("q_lo", [P, TILES, DK])
        q_t = sb("q_t", [DK, TILES, P])
        k_t = sb("k_t", [DK, S])
        top = sb("top", [P, TILES, CAND])
        idx = sb("idx", [P, TILES, CAND], U32)
        row_of = sb("row_of", [P, TILES, CAND], U32)
        base = sb("base", [P, 1])
        k_hi = sb("k_hi", [P, PC, DK])
        pa = sb("pa", [P, PC, DK])
        lanes = sb("lanes", [P, 4, PC, 4])
        pair = sb("pair", [P, PC, 2])
        w1 = sb("w1", [P, TILES, W])
        w2 = sb("w2", [P, TILES, W])
        wi = sb("wi", [P, TILES, W], I32)
        cand_tmp = sb("cand_tmp", [P, TILES, CAND])
        biases = sb("biases", [P, 3])
        stats = sb("stats", [P, 4, TILES])
        a_t = sb("a_t", [P, 2, 3, P])
        diag = sb("diag", [P, 2, CAND // 2, P])
        out = sb("out", [P, TILES, DK])
        ps = ctx.enter_context(nc.psum_tensor("b_ps", [P, 8, 512], F32))

        ident_ready = sem("ident_ready")
        loaded = [sem(f"loaded{j}") for j in range(2)]
        qk_psum = sem("qk_psum")
        qk_copied = sem("qk_copied")
        turn_psum = sem("turn_psum")
        turn_copied = sem("turn_copied")
        score_psum = sem("score_psum")
        score_copied = sem("score_copied")
        rows_ready = sem("rows_ready")
        gathered = [sem(f"gathered{i}") for i in range(2)]
        masked = sem("masked")
        trunc_ready = sem("trunc_ready")
        rest_ready = sem("rest_ready")
        dist_ready = sem("dist_ready")
        max_ready = sem("max_ready")
        exp_ready = sem("exp_ready")
        prob_ready = sem("prob_ready")
        turn_ready = sem("turn_ready")
        frac_ready = sem("frac_ready")
        wave_ready = sem("wave_ready")
        weights_ready = sem("weights_ready")
        diag_ready = sem("diag_ready")
        diag_used = sem("diag_used")
        pv_ready = sem("pv_ready")
        out_ready = sem("out_ready")
        out_free = sem("out_free")
        stored = sem("stored")
        small_ops = sem("small_ops")
        passed = sem("passed")

        def block_rows(t):
            return P if t == TILES - 1 else STRIDE

        def run(engine, step):
            step(0, 0, False, True)
            with engine.Fori(0, N // 2 - 1) as two:
                for i in range(2):
                    step(two * 2 + i + 1, 1 - i, True, True)
            step(N - 1, 1, True, False)
            step(N, 0, True, None)

        block = ctx.enter_context(nc.Block())

        @block.sync
        def _(sp):
            q_of = s["q"].rearrange("b h r d -> (b h) r d")
            kv_of = s["kv"].rearrange("b h r d -> (b h) r d")

            def load(n, j):
                for t in range(TILES):
                    at = slice(STRIDE * t, STRIDE * t + P)
                    for dst, src in ((q[:, j, t, :], q_of), (kv[:, j, t, :], kv_of)):
                        sp.dma_start(dst, src[bass.ds(n, 1), at, :].rearrange("o r d -> (o r) d")
                                     ).then_inc(loaded[j], 16)

            def store(n, j, more):
                if more:
                    sp.wait_ge(pv_ready, n * TILES + TILES)
                    load(n + 2, j)
                sp.wait_ge(out_ready, n + 1)
                dst = s["ctx"][bass.ds(n, 1), :, :].rearrange("o r d -> (o r) d")
                sp.dma_start(dst[0:STRIDE * TILES, :].rearrange("(t r) d -> r t d", t=TILES),
                             out[0:STRIDE, :, :]).then_inc(stored, 16)
                sp.dma_start(dst[S - TAIL:S, :], out[STRIDE:P, TILES - 1, :]).then_inc(stored, 16)
                sp.wait_ge(stored, n * 32 + 32)
                sp.sem_inc(out_free, 1)

            sp.sem_inc(out_free, 1)
            load(0, 0)
            load(1, 1)
            with sp.Fori(0, N // 2 - 1) as two:
                for j in range(2):
                    store(two * 2 + j, j, True)
            store(N - 2, 0, False)
            store(N - 1, 1, False)

        @block.gpsimd
        def _(gp):
            gp.memset(ident[:, :], 0.0)
            gp.memset(biases[:, 0:1], -1.0 / 3.0)
            gp.memset(biases[:, 1:2], math.pi / 2.0)
            gp.memset(biases[:, 2:3], -(0.5 - 2.0 ** -25))
            gp.memset(base[:, :], 0.0).then_inc(ident_ready, 1)
            gp.wait_ge(ident_ready, 1)
            gp.affine_select(out=ident[:, :], in_=ident[:, :], compare_op=ALU.not_equal, fill=1.0,
                             base=0, pattern=[[-1, P]], channel_multiplier=1).then_inc(ident_ready, 1)
            table = s["kv"].rearrange("b h r d -> (b h r) d")
            with gp.Fori(0, N // 2) as two:
                for j in range(2):
                    for half in range(2):
                        wait_alone(gp, rows_ready, two * 4 + j * 2 + half + 1, passed)
                        for i in range(TH * CAND):
                            at = half * TH * CAND + i
                            rows = row_of[:, at // CAND, at % CAND:at % CAND + 1]
                            gp.indirect_dma_start(kv_c[:, j, at, :], None, table,
                                                  bass.IndirectOffsetOnAxis(rows, 0)).then_inc(gathered[half], 16)

        @block.tensor
        def _(pe):
            def scores(m, j, count):
                wait_alone(pe, loaded[j], count * (2 * TILES * 16), passed)
                for g in range(4):
                    if g == 3:
                        wait_alone(pe, qk_copied, m * 4 + 1, passed)
                    for i in range(3):
                        t = 3 * (g % 2) + i
                        src = kv[:, j, t, 0:DK] if g < 2 else q[:, j, t, :]
                        mm = pe.transpose(ps[0:DK, 4 + g % 3, P * i:P * i + P], src, ident[:, :])
                    mm.then_inc(qk_psum, 1)
                pe.wait_ge(qk_copied, m * 4 + 4)
                for t in range(TILES):
                    if t >= 2:
                        pe.wait_ge(score_copied, m * TILES + t - 1)
                    for half in range(2):
                        mm = pe.matmul(ps[:, 2 * (t % 2) + half, 0:HALF], q_t[:, t, :],
                                       k_t[:, HALF * half:HALF * half + HALF], start=True, stop=True)
                    mm.then_inc(score_psum, 1)

            def weights_v(m, j):
                def turn(g):
                    t, part = g // 2, g % 2
                    if g >= 3:
                        pe.wait_ge(turn_copied, m * TURN_GROUPS + g - 2)
                    for i in range(3):
                        k = 3 * part + i
                        mm = pe.transpose(ps[0:block_rows(k), 4 + g % 3, P * i:P * i + P],
                                          sc[:, j, t, STRIDE * k:STRIDE * k + block_rows(k)], ident[:, :])
                    mm.then_inc(turn_psum, 1)

                def weigh(g):
                    t, part = g // 2, g % 2
                    pe.wait_ge(turn_copied, m * TURN_GROUPS + g + 1)
                    for i in range(3):
                        k = 3 * part + i
                        mm = pe.matmul(ps[:, 7, DK * t:DK * t + DK], a_t[0:block_rows(k), g % 2, i, :],
                                       kv[0:block_rows(k), j, k, DK:], start=(k == 0), stop=False)
                    pe.wait_ge(diag_ready, m * TURN_GROUPS + g + 1)
                    for i in range(CAND // 2):
                        c = CAND // 2 * part + i
                        mm = pe.matmul(ps[:, 7, DK * t:DK * t + DK], diag[:, part, i, :],
                                       kv_c[:, j, t * CAND + c, DK:], start=False, stop=(c == CAND - 1))
                    mm.then_inc(pv_ready if part else diag_used, 1)

                pe.wait_ge(weights_ready, m + 1)
                turn(0)
                for g in range(1, TURN_GROUPS):
                    turn(g)
                    weigh(g - 1)
                weigh(TURN_GROUPS - 1)

            pe.wait_ge(ident_ready, 2)
            scores(0, 0, 1)
            scores(1, 1, 1)
            with pe.Fori(0, N // 2 - 1) as two:
                for j in range(2):
                    m = two * 2 + j
                    weights_v(m, j)
                    scores(m + 2, j, two + 2)
            weights_v(N - 2, 0)
            weights_v(N - 1, 1)

        @block.scalar
        def _(act):
            def turned_qk(m):
                for g in range(4):
                    act.wait_ge(qk_psum, m * 4 + g + 1)
                    for i in range(3):
                        t = 3 * (g % 2) + i
                        if g < 2:
                            last = act.activation(k_t[:, STRIDE * t:STRIDE * t + block_rows(t)],
                                                  ps[0:DK, 4 + g % 3, P * i:P * i + block_rows(t)],
                                                  ACT.Copy, scale=DK ** -0.5)
                        elif i == 0:
                            last = act.activation(q_t[:, t:t + 3, :].rearrange("p t r -> p (t r)"),
                                                  ps[0:DK, 4 + g % 3, 0:3 * P], ACT.Copy)
                    last.then_inc(qk_copied, 1)

            def scores(m, j, half):
                for t in range(half * TH, half * TH + TH):
                    act.wait_ge(score_psum, m * TILES + t + 1)
                    act.activation(sc[:, j, t, 0:S].rearrange("p (a n) -> p a n", a=2),
                                   ps[:, 2 * (t % 2):2 * (t % 2) + 2, 0:HALF], ACT.Copy).then_inc(score_copied, 1)

            def turned_weights(m, j):
                for g in range(TURN_GROUPS):
                    t, part = g // 2, g % 2
                    act.wait_ge(turn_psum, m * TURN_GROUPS + g + 1)
                    if part == 0:
                        last = act.activation(a_t[0:STRIDE, g % 2, :, :], ps[0:STRIDE, 4 + g % 3, 0:3 * P]
                                              .rearrange("p (i n) -> p i n", i=3), ACT.Copy)
                    else:
                        act.activation(a_t[0:STRIDE, g % 2, 0:2, :], ps[0:STRIDE, 4 + g % 3, 0:2 * P]
                                       .rearrange("p (i n) -> p i n", i=2), ACT.Copy)
                        last = act.activation(a_t[:, g % 2, 2, :], ps[:, 4 + g % 3, 2 * P:3 * P], ACT.Copy)
                    last.then_inc(turn_copied, 1)
                    if t:
                        act.wait_ge(pv_ready if part else diag_used, m * TILES + t)
                    for i in range(CAND // 2):
                        c = S + CAND // 2 * part + i
                        last = act.activation(diag[:, part, i, :], ident[:, :], ACT.Copy, scale=sc[:, j, t, c:c + 1])
                    last.then_inc(diag_ready, 1)

            def step(n, j, before, after):
                if after is None:
                    turned_weights(n - 1, 1 - j)
                    return
                act.wait_ge(masked, n + 1)
                if before:
                    act.wait_ge(weights_ready, n)
                act.activation(w1[:, :, 0:S], sc[:, j, :, 0:S], ACT.Abs, scale=1618.0)
                act.drain()
                act.activation(wi[:, :, 0:S], w1[:, :, 0:S], ACT.Identity, scale=1.0 / 3.0,
                               bias=biases[:, 0:1]).then_inc(trunc_ready, 1)
                if before:
                    turned_weights(n - 1, 1 - j)
                act.wait_ge(rest_ready, n + 1)
                act.activation(w1[:, :, 0:S], w1[:, :, 0:S], ACT.Abs, bias=biases[:, 2:3]).then_inc(dist_ready, 1)
                if after:
                    turned_qk(n + 1)
                    scores(n + 1, 1 - j, 0)
                act.wait_ge(max_ready, n + 1)
                for t in range(TILES):
                    last = act.activation(w2[:, t, :], w2[:, t, :], ACT.Exp, bias=stats[:, 1, t:t + 1],
                                          accum_out=stats[:, 2, t:t + 1])
                last.then_inc(exp_ready, 1)
                if after:
                    scores(n + 1, 1 - j, 1)
                act.wait_ge(prob_ready, n + 1)
                act.activation(wi[:, :, :], w2[:, :, :], ACT.Copy, scale=TURNS).then_inc(turn_ready, 1)
                act.activation(sc[:, j, :, :], w2[:, :, :], ACT.Square)
                act.drain()
                act.activation(sc[:, j, :, :], sc[:, j, :, :], ACT.Exp, scale=-1.0 / PHI)
                for half in range(2):
                    act.wait_ge(frac_ready, n * 2 + half + 1)
                    at = slice(half * TH, half * TH + TH)
                    act.activation(w1[:, at, :], w1[:, at, :], ACT.Sin, scale=TWO_PI)
                    act.activation(wi[:, at, :].bitcast(F32), w2[:, at, :], ACT.Sin, scale=-COS,
                                   bias=biases[:, 1:2]).then_inc(wave_ready, 1)

            act.wait_ge(ident_ready, 2)
            turned_qk(0)
            scores(0, 0, 0)
            scores(0, 0, 1)
            run(act, step)

        @block.vector
        def _(dve):
            def largest(m, j, half):
                tiles = range(half * TH, half * TH + TH)
                at = slice(half * TH, half * TH + TH)
                wait_alone(dve, score_copied, m * TILES + half * TH + TH, passed)
                for t in tiles:
                    dve.max(top[:, t, :], sc[:, j, t, 0:S])
                dve.drain()
                for t in tiles:
                    dve.max_index(idx[:, t, :], top[:, t, :], sc[:, j, t, 0:S])
                dve.drain()
                dve.tensor_scalar(row_of[:, at, :], idx[:, at, :], base[:, :], None,
                                  ALU.add).then_inc(rows_ready, 1)
                dve.drain()

            def mask(j, half):
                for t in range(half * TH, half * TH + TH):
                    dve.match_replace(sc[:, j, t, 0:S], top[:, t, :], sc[:, j, t, 0:S], NEG)

            def next_base(count):
                dve.tensor_scalar(base[:, :], base[:, :], float(S), None, ALU.add).then_inc(masked, 1)

            def by_row(x, half):
                at = slice(half * TH * CAND, half * TH * CAND + TH * CAND)
                return x[:, at, :].rearrange("p (t c) d -> p t c d", c=CAND)

            def spread(x, half):
                return x[:, half * TH:half * TH + TH, :].unsqueeze(2).broadcast_to([P, TH, CAND, DK])

            def products(j, half):
                k = kv_c[:, j, :, 0:DK]
                part = slice(half * TH * CAND, half * TH * CAND + TH * CAND)
                k_part, hi, a = k[:, part, :], k_hi[:, part, :], pa[:, part, :]
                dve.tensor_scalar(hi.bitcast(I32), k_part.bitcast(I32), HIGH_BITS, None, ALU.bitwise_and)
                dve.tensor_tensor(by_row(pa, half), by_row(k, half), spread(q_lo, half), ALU.mult)
                dve.drain()
                dve.tensor_tensor(k_part, k_part, hi, ALU.subtract)
                dve.drain()
                dve.tensor_tensor(by_row(k, half), by_row(k, half), spread(q_hi, half), ALU.mult)
                dve.drain()
                dve.tensor_tensor(k_part, k_part, a, ALU.add)
                dve.drain()
                dve.tensor_tensor(by_row(pa, half), by_row(k_hi, half), spread(q_hi, half), ALU.mult)
                dve.drain()
                dve.tensor_scalar(hi, a, M_SCORE, M_SCORE, ALU.add, ALU.subtract)
                dve.drain()
                dve.tensor_tensor(a, a, hi, ALU.subtract)
                dve.drain()
                dve.tensor_tensor(a, a, k_part, ALU.add)

            acc, grid, low, high = (lanes[:, i, :, :] for i in range(4))

            def rounded_steps(n):
                def before_last(at):
                    if at >= 2:
                        dve.wait_ge(small_ops, n * SMALL_OPS + at - 1)

                halves = (slice(0, TH * CAND), slice(TH * CAND, PC))
                for i in range(4, DK, 4):
                    at = 10 * (i // 4 - 1)
                    for half, c in enumerate(halves):
                        before_last(at + half)
                        dve.tensor_scalar(grid[:, c], acc[:, c], M_SCORE, M_SCORE, ALU.add,
                                          ALU.subtract).then_inc(small_ops, 1)
                    for half, c in enumerate(halves):
                        before_last(at + 2 + half)
                        dve.tensor_tensor(low[:, c], acc[:, c], grid[:, c], ALU.subtract).then_inc(small_ops, 1)
                    for half, c in enumerate(halves):
                        before_last(at + 4 + half)
                        dve.tensor_tensor(high[:, c], grid[:, c], k_hi[:, c, i:i + 4],
                                          ALU.add).then_inc(small_ops, 1)
                    for half, c in enumerate(halves):
                        before_last(at + 6 + half)
                        dve.tensor_tensor(low[:, c], low[:, c], pa[:, c, i:i + 4], ALU.add).then_inc(small_ops, 1)
                    for half, c in enumerate(halves):
                        before_last(at + 8 + half)
                        dve.tensor_tensor(acc[:, c], high[:, c], low[:, c], ALU.add).then_inc(small_ops, 1)
                dve.drain()

            def candidate_filter(j):
                s_c, x, y, z = sc[:, j, :, S:W], w1[:, :, S:W], cand_tmp[:, :, :], wi[:, :, S:W]
                dve.tensor_tensor(pair[:, :, :], lanes[:, 0, :, 0:4:2], lanes[:, 0, :, 1:4:2], ALU.add)
                dve.drain()
                dve.tensor_tensor(pair[:, :, 0], pair[:, :, 0], pair[:, :, 1], ALU.add)
                dve.drain()
                dve.tensor_scalar(s_c, pair[:, :, 0].rearrange("p (t c) -> p t c", c=CAND), DK ** -0.5, None,
                                  ALU.mult)
                dve.drain()
                dve.tensor_scalar(y, s_c, -1.0, None, ALU.mult)
                dve.drain()
                dve.tensor_tensor(x, s_c, y, ALU.max)
                dve.drain()
                dve.tensor_scalar(x, x, 1618.0, None, ALU.mult)
                dve.drain()
                dve.tensor_scalar(z, x, 1.0 / 3.0, -1.0 / 3.0, ALU.mult, ALU.add)
                dve.drain()
                dve.scalar_tensor_tensor(x, z, -3.0, x, ALU.mult, ALU.add)
                dve.drain()
                dve.tensor_scalar(y, x, 0.0, None, ALU.is_lt)
                dve.drain()
                dve.scalar_tensor_tensor(x, x, 1.0, y, ALU.is_ge, ALU.max)
                dve.drain()
                dve.tensor_scalar(x, x, PHI_INV, None, ALU.max)

            def finish(m):
                dve.wait_ge(pv_ready, m * TILES + TILES)
                dve.wait_ge(out_free, m + 1)
                dve.tensor_copy(out[:, :, :], ps[:, 7, 0:TILES * DK]
                                .rearrange("p (t d) -> p t d", d=DK)).then_inc(out_ready, 1)

            def step(n, j, before, after):
                if after is None:
                    finish(n - 1)
                    return
                dve.tensor_scalar(q_hi[:, :, :].bitcast(I32), q[:, j, :, :].bitcast(I32), HIGH_BITS, None,
                                  ALU.bitwise_and)
                dve.drain()
                dve.tensor_tensor(q_lo[:, :, :], q[:, j, :, :], q_hi[:, :, :], ALU.subtract)
                dve.drain()
                for half in range(2):
                    dve.wait_ge(gathered[half], n * (TH * CAND * 16) + TH * CAND * 16)
                    products(j, half)
                dve.drain()
                dve.wait_ge(trunc_ready, n + 1)
                dve.scalar_tensor_tensor(w1[:, :, 0:S], wi[:, :, 0:S], -3.0, w1[:, :, 0:S], ALU.mult,
                                         ALU.add).then_inc(rest_ready, 1)
                dve.tensor_tensor(acc, k_hi[:, :, 0:4], pa[:, :, 0:4], ALU.add)
                dve.drain()
                rounded_steps(n)
                if before:
                    finish(n - 1)
                candidate_filter(j)
                dve.wait_ge(dist_ready, n + 1)
                dve.tensor_scalar(w1[:, :, 0:S], w1[:, :, 0:S], 0.5, PHI_INV, ALU.is_ge, ALU.max)
                dve.drain()
                for t in range(TILES):
                    dve.tensor_tensor_reduce(w2[:, t, :], w1[:, t, :], sc[:, j, t, :], 1.0, NEG, ALU.mult,
                                             ALU.max, stats[:, 0, t:t + 1])
                dve.drain()
                dve.tensor_scalar(stats[:, 1, :], stats[:, 0, :], -1.0, None, ALU.mult).then_inc(max_ready, 1)
                if after:
                    largest(n + 1, 1 - j, 0)
                dve.wait_ge(exp_ready, n + 1)
                dve.reciprocal(stats[:, 3, :], stats[:, 2, :])
                dve.drain()
                for t in range(TILES):
                    last = dve.tensor_scalar(w2[:, t, :], w2[:, t, :], stats[:, 3, t:t + 1], None, ALU.mult)
                last.then_inc(prob_ready, 1)
                if after:
                    largest(n + 1, 1 - j, 1)
                    mask(1 - j, 0)
                    mask(1 - j, 1)
                    next_base(1)
                dve.wait_ge(turn_ready, n + 1)
                for half in range(2):
                    at = slice(half * TH, half * TH + TH)
                    dve.scalar_tensor_tensor(w1[:, at, :], w2[:, at, :], TURNS, wi[:, at, :], ALU.mult,
                                             ALU.subtract).then_inc(frac_ready, 1)
                for half in range(2):
                    at = slice(half * TH, half * TH + TH)
                    dve.wait_ge(wave_ready, n * 2 + half + 1)
                    dve.tensor_tensor(w1[:, at, :], w1[:, at, :], sc[:, j, at, :], ALU.mult)
                    dve.drain()
                    dve.tensor_tensor(w1[:, at, :], w1[:, at, :], wi[:, at, :].bitcast(F32), ALU.add)
                    dve.drain()
                    last = dve.tensor_tensor(sc[:, j, at, :], w1[:, at, :], w2[:, at, :], ALU.mult)
                last.then_inc(weights_ready, 1)
                dve.drain()

            dve.wait_ge(ident_ready, 2)
            largest(0, 0, 0)
            largest(0, 0, 1)
            mask(0, 0)
            mask(0, 1)
            next_base(1)
            run(dve, step)


def experts(nc, a, s, out):
    with ExitStack() as ctx:
        def sb(name, shape, dt=F32):
            return ctx.enter_context(nc.sbuf_tensor("c_" + name, shape, dt))

        def sem(name):
            return ctx.enter_context(nc.semaphore("c_" + name))

        KB = LAT // P
        ROWS = TILES * P
        BANK = 512
        ident = sb("ident", [P, P])
        ones = sb("ones", [1, P])
        w_o = sb("w_o", [P, KB, D])
        w_r = sb("w_r", [D, EXPERTS])
        w_1 = sb("w_1", [D, EXPERTS, HID])
        w_2 = sb("w_2", [HID, EXPERTS, D])
        b_1 = sb("b_1", [HID, EXPERTS])
        b_2 = sb("b_2", [1, EXPERTS * D])
        vec = sb("vec", [P, 3, D])
        b_r = sb("b_r", [P, EXPERTS])
        slots = sb("slots", [P, EXPERTS])
        h = sb("h", [P, 2, TILES, D])
        heads = sb("heads", [P, 2, TILES, LAT])
        heads_t = sb("heads_t", [P, 2, KB, P])
        res = sb("res", [P, TILES, D])
        x2 = sb("x2", [P, TILES, D])
        xn = sb("xn", [P, TILES, D])
        xn_t = sb("xn_t", [D, ROWS])
        stats = sb("stats", [P, TILES, 6])
        agg = sb("agg", [P, TILES, 2])
        col = sb("col", [P, 8, TILES])
        logits = sb("logits", [P, TILES, EXPERTS])
        top = sb("top", [P, TILES, 8])
        top_i = sb("top_i", [P, TILES, 8], U32)
        top_f = sb("top_f", [P, TILES, 2])
        gate = sb("gate", [P, TILES, EXPERTS])
        gate2 = sb("gate2", [P, TILES, EXPERTS])
        hid = sb("hid", [HID, EXPERTS, ROWS])
        mix = sb("mix", [P, 2, EXPERTS, D])
        y = sb("y", [P, TILES, D])
        y_out = sb("y_out", [P, TILES, D])
        ps = ctx.enter_context(nc.psum_tensor("c_ps", [P, 8, BANK], F32))
        ps_o = ps[:, 2, 0:TILES * D]
        ps_x = ps[0:D, 3:5, :].rearrange("p a n -> p (a n)")[:, 0:ROWS]
        ps_r = ps[:, 4, BANK - TILES * EXPERTS:BANK]
        assert ROWS <= 2 * BANK - TILES * EXPERTS

        def ps_h(e):
            at = 5 if e % 2 == 0 else 0
            return ps[:, at:at + 2, :].rearrange("p a n -> p (a n)")

        def ps_y(t):
            return ps[:, 7 if t % 2 == 0 else 3, :]

        consts_in = sem("consts_in")
        ident_ready = sem("ident_ready")
        rows_in = [sem(f"rows_in{j}") for j in range(2)]
        rows_used = sem("rows_used")
        heads_psum = sem("heads_psum")
        heads_ready = sem("heads_ready")
        proj_ready = sem("proj_ready")
        var_ready = sem("var_ready")
        root_ready = sem("root_ready")
        xn_ready = sem("xn_ready")
        xt_psum = sem("xt_psum")
        xt_ready = sem("xt_ready")
        logits_psum = sem("logits_psum")
        hid_psum = sem("hid_psum")
        hid_ready = sem("hid_ready")
        gap_ready = sem("gap_ready")
        odds_ready = sem("odds_ready")
        y_psum = sem("y_psum")
        tiles_mixed = sem("tiles_mixed")
        y_ready = sem("y_ready")
        out_free = sem("out_free")
        stored = sem("stored")
        passed = sem("passed")

        block = ctx.enter_context(nc.Block())

        @block.sync
        def _(sp):
            for dst, src in ((w_o[:, :, :], a["Wo"].rearrange("(k p) d -> p k d", p=P)),
                             (w_r[:, :], a["Wr"]),
                             (w_1[:, :, :], a["W1"].rearrange("e d h -> d e h")),
                             (w_2[:, :, :], a["W2"].rearrange("e h d -> h e d")),
                             (b_1[:, :], a["b1_t"]),
                             (b_2[:, :], a["b2"].rearrange("(o e) d -> o (e d)", o=1)),
                             (vec[:, 0, :], a["bo"].partition_broadcast(P)),
                             (vec[:, 1, :], a["gamma"].partition_broadcast(P)),
                             (vec[:, 2, :], a["beta2"].partition_broadcast(P)),
                             (b_r[:, :], a["br"].partition_broadcast(P))):
                sp.dma_start(dst, src).then_inc(consts_in, 16)
            sp.sem_inc(out_free, 1)
            with sp.Fori(0, B) as b:
                sp.wait_ge(y_ready, b + 1)
                sp.dma_start(out[b, 0:STRIDE * TILES, :].rearrange("(t r) d -> r t d", t=TILES),
                             y_out[0:STRIDE, :, :]).then_inc(stored, 16)
                sp.dma_start(out[b, S - TAIL:S, :], y_out[STRIDE:P, TILES - 1, :]).then_inc(stored, 16)
                sp.wait_ge(stored, b * 32 + 32)
                sp.sem_inc(out_free, 1)

        @block.gpsimd
        def _(gp):
            gp.memset(ident[:, :], 0.0)
            gp.memset(ones[:, :], 1.0)
            gp.iota(slots[:, :], pattern=[[1, EXPERTS]], base=0, channel_multiplier=0,
                    allow_small_or_imprecise_dtypes=True).then_inc(ident_ready, 1)
            gp.wait_ge(ident_ready, 1)
            gp.affine_select(out=ident[:, :], in_=ident[:, :], compare_op=ALU.not_equal, fill=1.0,
                             base=0, pattern=[[-1, P]], channel_multiplier=1).then_inc(ident_ready, 1)
            with gp.Fori(0, B // 2) as two:
                for j in range(2):
                    b = two * 2 + j
                    gp.wait_ge(rows_used, b + 1)
                    for t in range(TILES):
                        at = slice(t * STRIDE, t * STRIDE + P)
                        gp.dma_start(h[:, j, t, :], s["h"][bass.ds(b, 1), at, :]
                                     .rearrange("o r d -> (o r) d")).then_inc(rows_in[j], 16)
                        gp.dma_start(heads[:, j, t, :].rearrange("r (h d) -> r h d", h=HEADS),
                                     s["ctx"][bass.ds(b * HEADS, HEADS), at, :]
                                     .rearrange("h r d -> r h d")).then_inc(rows_in[j], 16)

        @block.tensor
        def _(pe):
            def turn_heads(b, j, t):
                for k in range(KB):
                    mm = pe.transpose(ps[:, t % 2, P * k:P * k + P], heads[:, j, t, P * k:P * k + P], ident[:, :])
                mm.then_inc(heads_psum, 1)

            def project(b, t):
                pe.wait_ge(heads_ready, b * TILES + t + 1)
                for k in range(KB):
                    mm = pe.matmul(ps_o[:, D * t:D * t + D], heads_t[:, t % 2, k, :], w_o[:, k, :],
                                   start=(k == 0), stop=(k == KB - 1))
                return mm

            def batch(b, j, count):
                pe.wait_ge(rows_in[j], count * (TILES * 32))
                turn_heads(b, j, 0)
                for t in range(1, TILES):
                    turn_heads(b, j, t)
                    project(b, t - 1)
                project(b, TILES - 1).then_inc(proj_ready, 1)
                wait_alone(pe, xn_ready, b + 1, passed)
                for t in range(TILES):
                    mm = pe.transpose(ps_x[:, P * t:P * t + P], xn[:, t, :], ident[:, :])
                mm.then_inc(xt_psum, 1)
                pe.wait_ge(xt_ready, b + 1)
                for t in range(TILES):
                    mm = pe.matmul(ps_r[:, EXPERTS * t:EXPERTS * t + EXPERTS], xn_t[:, P * t:P * t + P], w_r[:, :],
                                   start=True, stop=True)
                mm.then_inc(logits_psum, 1)
                for e in range(EXPERTS):
                    if e >= 2:
                        pe.wait_ge(hid_ready, b * EXPERTS + e - 1)
                    for at in range(0, ROWS, BANK):
                        to = min(at + BANK, ROWS)
                        mm = pe.matmul(ps_h(e)[:, at:to], w_1[:, e, :], xn_t[:, at:to], start=True, stop=True)
                    mm.then_inc(hid_psum, 1)
                pe.wait_ge(hid_ready, b * EXPERTS + EXPERTS)
                for t in range(TILES):
                    if t >= 2:
                        pe.wait_ge(tiles_mixed, b * TILES + t - 1)
                    pe.matmul(ps_y(t), ones[:, :], b_2[:, :], start=True, stop=False, skip_group_check=True)
                    for e in range(EXPERTS):
                        mm = pe.matmul(ps_y(t)[:, D * e:D * e + D], hid[:, e, P * t:P * t + P], w_2[:, e, :],
                                       start=False, stop=(e == EXPERTS - 1), skip_group_check=True)
                    mm.then_inc(y_psum, 1)

            pe.wait_ge(ident_ready, 2)
            pe.wait_ge(consts_in, 160)
            with pe.Fori(0, B // 2) as two:
                for j in range(2):
                    batch(two * 2 + j, j, two + 1)

        @block.scalar
        def _(act):
            act.wait_ge(consts_in, 160)
            with act.Fori(0, B) as b:
                for t in range(TILES):
                    act.wait_ge(heads_psum, b * TILES + t + 1)
                    act.activation(heads_t[:, t % 2, :, :].rearrange("p k n -> p (k n)"), ps[:, t % 2, :],
                                   ACT.Copy).then_inc(heads_ready, 1)
                for i in range(2):
                    act.wait_ge(var_ready, b * 2 + i + 1)
                    act.activation(col[:, 1, :], col[:, 0, :], ACT.Sqrt).then_inc(root_ready, 1)
                act.wait_ge(xt_psum, b + 1)
                act.activation(xn_t[:, :], ps_x, ACT.Copy).then_inc(xt_ready, 1)
                for e in range(EXPERTS):
                    act.wait_ge(hid_psum, b * EXPERTS + e + 1)
                    act.activation(hid[:, e, :], ps_h(e)[:, 0:ROWS], ACT.Gelu,
                                   bias=b_1[:, e:e + 1]).then_inc(hid_ready, 1)
                act.wait_ge(gap_ready, b + 1)
                act.activation(col[:, 5, :], col[:, 4, :], ACT.Exp).then_inc(odds_ready, 1)

        @block.vector
        def _(dve):
            def c(i):
                return col[:, i, :]

            def all_tiles(x, n):
                return x.unsqueeze(1).broadcast_to([P, TILES, n])

            def norm(dst, src, count):
                for t in range(TILES):
                    dve.bn_stats(stats[:, t, :], src[:, t, :])
                dve.drain()
                for t in range(TILES):
                    dve.bn_aggr(agg[:, t, :], stats[:, t, :])
                dve.drain()
                dve.tensor_scalar(c(0), agg[:, :, 1], LN_EPS, None, ALU.add).then_inc(var_ready, 1)
                dve.wait_ge(root_ready, count)
                dve.reciprocal(c(2), c(1))
                dve.drain()
                dve.tensor_tensor(c(2), c(2), c(0), ALU.mult)
                dve.drain()
                dve.tensor_tensor(c(2), c(2), c(1), ALU.add)
                dve.drain()
                dve.tensor_scalar(c(2), c(2), 0.5, None, ALU.mult)
                dve.drain()
                dve.reciprocal(c(3), c(2))
                dve.drain()
                for t in range(TILES):
                    dve.tensor_scalar(dst[:, t, :], src[:, t, :], agg[:, t, 0:1], col[:, 3, t:t + 1],
                                      ALU.subtract, ALU.mult)
                dve.drain()

            def batch(b, j, count):
                dve.wait_ge(proj_ready, b + 1)
                dve.tensor_tensor(res[:, :, :], ps_o.rearrange("p (t d) -> p t d", d=D), all_tiles(vec[:, 0, :], D),
                                  ALU.add)
                dve.drain()
                dve.wait_ge(rows_in[j], count * (TILES * 32))
                dve.tensor_tensor(res[:, :, :], res[:, :, :], h[:, j, :, :], ALU.add).then_inc(rows_used, 1)
                dve.drain()
                norm(x2, res, b * 2 + 1)
                norm(xn, x2, b * 2 + 2)
                dve.tensor_tensor(xn[:, :, :], xn[:, :, :], all_tiles(vec[:, 1, :], D), ALU.mult)
                dve.drain()
                dve.tensor_tensor(xn[:, :, :], xn[:, :, :], all_tiles(vec[:, 2, :], D), ALU.add).then_inc(xn_ready, 1)
                dve.wait_ge(logits_psum, b + 1)
                dve.tensor_tensor(logits[:, :, :], ps_r.rearrange("p (t e) -> p t e", e=EXPERTS),
                                  all_tiles(b_r[:, :], EXPERTS), ALU.add)
                dve.drain()
                for t in range(TILES):
                    dve.max(top[:, t, :], logits[:, t, :])
                dve.drain()
                for t in range(TILES):
                    dve.max_index(top_i[:, t, :], top[:, t, :], logits[:, t, :])
                dve.tensor_tensor(c(4), top[:, :, 1], top[:, :, 0], ALU.subtract).then_inc(gap_ready, 1)
                dve.drain()
                dve.tensor_copy(top_f[:, :, :], top_i[:, :, 0:2])
                dve.wait_ge(odds_ready, b + 1)
                dve.tensor_scalar(c(6), c(5), 1.0, None, ALU.add)
                dve.drain()
                dve.reciprocal(c(6), c(6))
                dve.drain()
                dve.tensor_tensor(c(7), c(5), c(6), ALU.mult)
                dve.drain()
                for t in range(TILES):
                    dve.tensor_scalar(gate[:, t, :], slots[:, :], top_f[:, t, 0:1], col[:, 6, t:t + 1],
                                      ALU.is_equal, ALU.mult)
                    dve.tensor_scalar(gate2[:, t, :], slots[:, :], top_f[:, t, 1:2], col[:, 7, t:t + 1],
                                      ALU.is_equal, ALU.mult)
                dve.drain()
                dve.tensor_tensor(gate[:, :, :], gate[:, :, :], gate2[:, :, :], ALU.add)
                dve.drain()
                for t in range(TILES):
                    dve.wait_ge(y_psum, b * TILES + t + 1)
                    dve.tensor_tensor(mix[:, t % 2, :, :], ps_y(t).rearrange("p (e d) -> p e d", e=EXPERTS),
                                      gate[:, t, :].unsqueeze(2).broadcast_to([P, EXPERTS, D]),
                                      ALU.mult).then_inc(tiles_mixed, 1)
                    dve.drain()
                    dve.tensor_reduce(y[:, t, :], mix[:, t % 2, :, :].rearrange("p e d -> p d e"), AX.X, ALU.add)
                dve.drain()
                dve.wait_ge(out_free, b + 1)
                dve.tensor_tensor(y_out[:, :, :], y[:, :, :], res[:, :, :], ALU.add).then_inc(y_ready, 1)
                dve.drain()

            dve.wait_ge(ident_ready, 2)
            dve.wait_ge(consts_in, 160)
            dve.sem_inc(rows_used, 2)
            with dve.Fori(0, B // 2) as two:
                for j in range(2):
                    batch(two * 2 + j, j, two + 1)


def build(nc, a, out):
    s = {"h": nc.dram_tensor("h", (B, S, D), F32, kind="Internal").ap(),
         "q": nc.dram_tensor("q", (B, HEADS, S, DK), F32, kind="Internal").ap(),
         "kv": nc.dram_tensor("kv", (B, HEADS, S, 2 * DK), F32, kind="Internal").ap(),
         "ctx": nc.dram_tensor("ctx", (B * HEADS, S, DK), F32, kind="Internal").ap()}
    tokens_and_projections(nc, a, s)
    attention(nc, s)
    experts(nc, a, s, out)


def kernel(x, L0_tok_kernel, L0_tok_bias, L0_tok_beta, L0_tok_moving_mean, L0_tok_moving_var,
           L0_attn_Wq, L0_attn_bq, L0_attn_Wk, L0_attn_bk, L0_attn_Wv, L0_attn_bv, L0_attn_Wo, L0_attn_bo,
           L0_ffn_gamma, L0_ffn_beta, L0_ffn_Wr, L0_ffn_br, L0_ffn_W1, L0_ffn_b1, L0_ffn_W2, L0_ffn_b2):
    from concourse import bacc
    from concourse.bass_utils import run_bass_kernel_spmd

    x_t = np.asarray(x).transpose(0, 2, 1)
    x_tiles = np.stack([x_t[b, :, STRIDE * t:STRIDE * t + P + TAPS - 1] for b in range(B) for t in range(TILES)])
    arrays = {
        "x_tiles": x_tiles, "kernel": L0_tok_kernel, "bias": L0_tok_bias, "beta": L0_tok_beta,
        "moving_mean": L0_tok_moving_mean, "moving_var": L0_tok_moving_var,
        "Wq": L0_attn_Wq, "bq": L0_attn_bq, "Wk": L0_attn_Wk, "bk": L0_attn_bk, "Wv": L0_attn_Wv,
        "bv": L0_attn_bv, "Wo": L0_attn_Wo, "bo": L0_attn_bo, "gamma": L0_ffn_gamma, "beta2": L0_ffn_beta,
        "Wr": L0_ffn_Wr, "br": L0_ffn_br, "W1": L0_ffn_W1, "b1_t": np.asarray(L0_ffn_b1).T,
        "W2": L0_ffn_W2, "b2": L0_ffn_b2,
    }
    arrays = {name: np.ascontiguousarray(v) for name, v in arrays.items()}
    nc = bacc.Bacc("TRN2", target_bir_lowering=False, num_devices=1)
    a = {name: nc.dram_tensor("in_" + name, v.shape, mybir.dt.from_np(v.dtype), kind="ExternalInput").ap()
         for name, v in arrays.items()}
    out = nc.dram_tensor("out", (B, S, D), F32, kind="ExternalOutput").ap()
    build(nc, a, out)
    got = run_bass_kernel_spmd(nc, [{"in_" + name: v for name, v in arrays.items()}], core_ids=[0])
    return got.results[0]["out"]
```
